# Optimizing a Trainium2 kernel written in Bass

```python
import numpy as np
import jax
import jax.numpy as jnp

def _softmax(x, axis=-1):
    return jax.nn.softmax(x, axis=axis)

def _gelu(x):
    return jax.nn.gelu(x, approximate=True)

def _silu(x):
    return jax.nn.silu(x)

def _sigmoid(x):
    return jax.nn.sigmoid(x)

def _layernorm(x, axis=-1, eps=1e-05):
    m = jnp.mean(x, axis=axis, keepdims=True)
    v = jnp.var(x, axis=axis, keepdims=True)
    return (x - m) / jnp.sqrt(v + eps)

def _scatter_add(tgt, idx, src, axis=0):
    return tgt.at[idx].add(src)

def _segment_sum(src, seg, n):
    return jax.ops.segment_sum(src, seg, n)
kernel_name = 'mk_gnn_preln_d4_gnn_r16_7553ea'

def setup_inputs(seed: int=0):
    np.random.seed(seed)
    _w = jnp.asarray

    def _rec_inputs():
        import jax
        import jax.numpy as jnp
        _gk = jax.random.key(seed)
        x = -0.0005121 + 1.001 * jax.random.normal(jax.random.fold_in(_gk, 1), (6250, 32), jnp.float32)
        src = jax.random.randint(jax.random.fold_in(_gk, 2), (100000,), 0, 6250, jnp.int32)
        dst = jnp.minimum((6250 * jax.random.uniform(jax.random.fold_in(_gk, 3), (100000,)) ** 2.0).astype(jnp.int32), 99999)
        _o = jnp.argsort(dst, stable=True)
        src = src[_o]
        dst = dst[_o]
        edge_attr3_2x32 = -8.16379e-05 + 0.999858 * jax.random.normal(jax.random.fold_in(_gk, 12), (100000, 2, 32), jnp.float32)
        edge_attr_2 = -5.09086e-05 + 0.577461 * jax.random.normal(jax.random.fold_in(_gk, 13), (100000, 2), jnp.float32)
        edge_attr_3 = jax.random.uniform(jax.random.fold_in(_gk, 14), (100000, 3), jnp.float32, 0.0, 0.999998)
        return (x, src, dst, edge_attr3_2x32, edge_attr_2, edge_attr_3)
    x, src, dst, edge_attr3_2x32, edge_attr_2, edge_attr_3 = _rec_inputs()

    def _L0_gnn_setup():
        import jax, jax.numpy as jnp
        import numpy as np
        N_NODES = 6250

        def gin_conv(x, src, dst, W1, b1, W2, b2):
            agg = jax.ops.segment_sum(x[src], dst, num_segments=N_NODES)
            h = x + agg
            h = jax.nn.relu(h @ W1 + b1)
            return h @ W2 + b2
        key = jax.random.key(seed)
        ks = jax.random.split(key, 10)
        N, E = (N_NODES, 100000)
        C_IN, C_H, C_OUT = (32, 64, 32)
        s = 0.05
        x = jax.random.normal(ks[0], (N, C_IN), dtype=jnp.float32)
        edge_index = jax.random.randint(ks[1], (2, E), 0, N, dtype=jnp.int64)
        return {'x': x, 'edge_index': edge_index, 'W1a': jax.random.normal(ks[2], (C_IN, C_H), dtype=jnp.float32) * s, 'b1a': jnp.zeros((C_H,), dtype=jnp.float32), 'W2a': jax.random.normal(ks[3], (C_H, C_H), dtype=jnp.float32) * s, 'b2a': jnp.zeros((C_H,), dtype=jnp.float32), 'W1b': jax.random.normal(ks[4], (C_H, C_H), dtype=jnp.float32) * s, 'b1b': jnp.zeros((C_H,), dtype=jnp.float32), 'W2b': jax.random.normal(ks[5], (C_H, C_OUT), dtype=jnp.float32) * s, 'b2b': jnp.zeros((C_OUT,), dtype=jnp.float32)}
    _L0_gnn_all = _L0_gnn_setup()
    _L0_gnn_in = {k: v for k, v in _L0_gnn_all.items() if k in ('W1a', 'b1a', 'W2a', 'b2a', 'W1b', 'b1b', 'W2b', 'b2b')}
    del _L0_gnn_all

    def _L1_gnn_setup():
        import jax, jax.numpy as jnp
        import numpy as np
        N = 3125
        E = 100000
        H = 2
        F = 32
        IN = 32
        OUT = 32
        NEG_SLOPE = 0.2
        key = jax.random.key(seed)
        ks = jax.random.split(key, 11)
        s = 0.1
        return {'feat': jax.random.normal(ks[0], (N, IN), jnp.float32), 'r_feat': jax.random.normal(ks[1], (E, H, F), jnp.float32), 'src': jax.random.randint(ks[2], (E,), 0, N), 'dst': jax.random.randint(ks[3], (E,), 0, N), 'W1': jax.random.normal(ks[4], (IN, OUT), jnp.float32) * s, 'b1': jnp.zeros((OUT,), jnp.float32), 'W2s': jax.random.normal(ks[5], (IN, H * F), jnp.float32) * s, 'b2s': jnp.zeros((H * F,), jnp.float32), 'W2d': jax.random.normal(ks[6], (IN, H * F), jnp.float32) * s, 'b2d': jnp.zeros((H * F,), jnp.float32), 'attn': jax.random.normal(ks[7], (1, H, F), jnp.float32) * s}
    _L1_gnn_all = _L1_gnn_setup()
    _L1_gnn_in = {k: v for k, v in _L1_gnn_all.items() if k in ('W1', 'b1', 'W2s', 'b2s', 'W2d', 'b2d', 'attn')}
    del _L1_gnn_all

    def _L2_gnn_setup():
        import jax, jax.numpy as jnp
        import numpy as np
        N_NODES = 3125
        N_EDGES = 100000
        F_IN = 32
        F_OUT = 32
        BASIS = (4, 4)

        def _tent_basis(u, n):
            centers = jnp.linspace(-1.0, 1.0, n, dtype=u.dtype)
            h = 2.0 / (n - 1)
            return jnp.maximum(0.0, 1.0 - jnp.abs(u[:, None] - centers[None, :]) / h)
        key = jax.random.key(seed)
        k1, k2, k3, k4, k5 = jax.random.split(key, 5)
        x = jax.random.normal(k1, (N_NODES, F_IN), dtype=jnp.float32)
        edge_attr = jax.random.uniform(k2, (N_EDGES, 2), dtype=jnp.float32, minval=-1.0, maxval=1.0)
        weight = jax.random.uniform(k3, (*BASIS, F_IN, F_OUT), dtype=jnp.float32, minval=-0.05, maxval=0.05)
        src = jax.random.randint(k4, (N_EDGES,), 0, N_NODES)
        tgt = jax.random.randint(k5, (N_EDGES,), 0, N_NODES)
        edge_index = jnp.stack([tgt, src], axis=0).astype(jnp.int64)
        return {'x': x, 'edge_attr': edge_attr, 'weight': weight, 'edge_index': edge_index}
    _L2_gnn_all = _L2_gnn_setup()
    _L2_gnn_in = {k: v for k, v in _L2_gnn_all.items() if k in ('weight',)}
    del _L2_gnn_all

    def _L3_gnn_setup():
        import jax, jax.numpy as jnp
        import numpy as np
        D = 3
        KS = 5
        K = KS ** D
        S = 2 ** D
        _COMBOS = np.array([[s >> d & 1 for d in range(D)] for s in range(S)], dtype=np.int32)
        _STRIDES = np.array([KS ** (D - 1 - d) for d in range(D)], dtype=np.int32)

        def spline_basis(pseudo):
            pos = pseudo * (KS - 1)
            i0 = jnp.clip(jnp.floor(pos), 0, KS - 2).astype(jnp.int32)
            frac = pos - i0
            combos = jnp.asarray(_COMBOS)
            basis = jnp.prod(jnp.where(combos[None] == 1, frac[:, None, :], 1.0 - frac[:, None, :]), axis=-1)
            idx = jnp.sum((i0[:, None, :] + combos[None]) * jnp.asarray(_STRIDES)[None, None, :], axis=-1)
            return (basis, idx)

        def spline_conv(x, row, col, basis, idx, W, b):
            N = x.shape[0]
            Fout = W.shape[2]
            z = jnp.einsum('ni,kio->nko', x, W).reshape(N * K, Fout)
            gathered = z[col[:, None] * K + idx]
            msg = jnp.einsum('es,eso->eo', basis, gathered)
            out = jax.ops.segment_sum(msg, row, num_segments=N)
            deg = jax.ops.segment_sum(jnp.ones_like(msg[:, 0]), row, num_segments=N)
            return out / jnp.maximum(deg, 1.0)[:, None] + b
        key = jax.random.key(seed)
        ks = jax.random.split(key, 13)
        N, E, Fin, Fout = (1250, 20000, 32, 32)

        def u(k, shape, size):
            bound = 1.0 / np.sqrt(size)
            return jax.random.uniform(k, shape, jnp.float32, -bound, bound)
        return dict(x=jax.random.normal(ks[0], (N, Fin), jnp.float32), edge_index=jax.random.randint(ks[1], (2, E), 0, N, dtype=jnp.int32), pseudo=jax.random.uniform(ks[2], (E, D), jnp.float32), stn1_w=u(ks[3], (K, 1, 64), 1 * S), stn1_b=u(ks[4], (64,), 1 * S), stn2_w=u(ks[5], (K, 64, 64), 64 * S), stn2_b=u(ks[6], (64,), 64 * S), stn3_w=u(ks[7], (64, 64), 64), stn3_b=u(ks[8], (64,), 64), stn4_w=u(ks[9], (64, 3), 64), stn4_b=u(ks[10], (3,), 64), conv_w=u(ks[11], (K, Fin, Fout), Fin * S), conv_b=u(ks[12], (Fout,), Fin * S))
    _L3_gnn_all = _L3_gnn_setup()
    _L3_gnn_in = {k: v for k, v in _L3_gnn_all.items() if k in ('stn1_w', 'stn1_b', 'stn2_w', 'stn2_b', 'stn3_w', 'stn3_b', 'stn4_w', 'stn4_b', 'conv_w', 'conv_b')}
    del _L3_gnn_all
    return {'x': x, 'src': src, 'dst': dst, 'edge_attr3_2x32': edge_attr3_2x32, 'edge_attr_2': edge_attr_2, 'edge_attr_3': edge_attr_3, 'L0_gnn_W1a': _L0_gnn_in['W1a'], 'L0_gnn_b1a': _L0_gnn_in['b1a'], 'L0_gnn_W2a': _L0_gnn_in['W2a'], 'L0_gnn_b2a': _L0_gnn_in['b2a'], 'L0_gnn_W1b': _L0_gnn_in['W1b'], 'L0_gnn_b1b': _L0_gnn_in['b1b'], 'L0_gnn_W2b': _L0_gnn_in['W2b'], 'L0_gnn_b2b': _L0_gnn_in['b2b'], 'L1_gnn_W1': _L1_gnn_in['W1'], 'L1_gnn_b1': _L1_gnn_in['b1'], 'L1_gnn_W2s': _L1_gnn_in['W2s'], 'L1_gnn_b2s': _L1_gnn_in['b2s'], 'L1_gnn_W2d': _L1_gnn_in['W2d'], 'L1_gnn_b2d': _L1_gnn_in['b2d'], 'L1_gnn_attn': _L1_gnn_in['attn'], 'L2_gnn_weight': _L2_gnn_in['weight'], 'L3_gnn_stn1_w': _L3_gnn_in['stn1_w'], 'L3_gnn_stn1_b': _L3_gnn_in['stn1_b'], 'L3_gnn_stn2_w': _L3_gnn_in['stn2_w'], 'L3_gnn_stn2_b': _L3_gnn_in['stn2_b'], 'L3_gnn_stn3_w': _L3_gnn_in['stn3_w'], 'L3_gnn_stn3_b': _L3_gnn_in['stn3_b'], 'L3_gnn_stn4_w': _L3_gnn_in['stn4_w'], 'L3_gnn_stn4_b': _L3_gnn_in['stn4_b'], 'L3_gnn_conv_w': _L3_gnn_in['conv_w'], 'L3_gnn_conv_b': _L3_gnn_in['conv_b']}

def reference(x, src, dst, edge_attr3_2x32, edge_attr_2, edge_attr_3, L0_gnn_W1a, L0_gnn_b1a, L0_gnn_W2a, L0_gnn_b2a, L0_gnn_W1b, L0_gnn_b1b, L0_gnn_W2b, L0_gnn_b2b, L1_gnn_W1, L1_gnn_b1, L1_gnn_W2s, L1_gnn_b2s, L1_gnn_W2d, L1_gnn_b2d, L1_gnn_attn, L2_gnn_weight, L3_gnn_stn1_w, L3_gnn_stn1_b, L3_gnn_stn2_w, L3_gnn_stn2_b, L3_gnn_stn3_w, L3_gnn_stn3_b, L3_gnn_stn4_w, L3_gnn_stn4_b, L3_gnn_conv_w, L3_gnn_conv_b):
    import jax
    import jax.numpy as jnp

    def _L0_gnn_ref(x, edge_index, W1a, b1a, W2a, b2a, W1b, b1b, W2b, b2b):
        import jax, jax.numpy as jnp
        import numpy as np
        N_NODES = 6250

        def gin_conv(x, src, dst, W1, b1, W2, b2):
            agg = jax.ops.segment_sum(x[src], dst, num_segments=N_NODES)
            h = x + agg
            h = jax.nn.relu(h @ W1 + b1)
            return h @ W2 + b2
        src, dst = (edge_index[0], edge_index[1])
        h = gin_conv(x, src, dst, W1a, b1a, W2a, b2a)
        h = jax.nn.relu(h)
        out = gin_conv(h, src, dst, W1b, b1b, W2b, b2b)
        return out

    def _L1_gnn_ref(feat, r_feat, src, dst, W1, b1, W2s, b2s, W2d, b2d, attn):
        import jax, jax.numpy as jnp
        import numpy as np
        N = 3125
        E = 100000
        H = 2
        F = 32
        IN = 32
        OUT = 32
        NEG_SLOPE = 0.2
        n = feat.shape[0]
        feat_src = (feat @ W2s + b2s).reshape(n, H, F)
        feat_dst = (feat @ W2d + b2d).reshape(n, H, F)
        en = feat_src[src]
        ev = feat_dst[dst]
        e = jax.nn.leaky_relu(en + ev, negative_slope=NEG_SLOPE)
        e = jnp.sum(e * attn, axis=-1, keepdims=True)
        m = jax.ops.segment_max(e, dst, num_segments=n)
        m = jnp.where(jnp.isfinite(m), m, 0.0)
        ee = jnp.exp(e - m[dst])
        denom = jax.ops.segment_sum(ee, dst, num_segments=n)
        alpha = ee / jnp.maximum(denom[dst], 1e-09)
        msg = jax.nn.softmax(en * r_feat * alpha, axis=-1)
        g_agg = jax.ops.segment_sum(msg, dst, num_segments=n)
        g_sum = jnp.sum(g_agg, axis=1)
        rst = (feat + g_sum) @ W1 + b1
        return rst

    def _L2_gnn_ref(x, edge_attr, weight, edge_index):
        import jax, jax.numpy as jnp
        import numpy as np
        N_NODES = 3125
        N_EDGES = 100000
        F_IN = 32
        F_OUT = 32
        BASIS = (4, 4)

        def _tent_basis(u, n):
            centers = jnp.linspace(-1.0, 1.0, n, dtype=u.dtype)
            h = 2.0 / (n - 1)
            return jnp.maximum(0.0, 1.0 - jnp.abs(u[:, None] - centers[None, :]) / h)
        k1, k2, f_in, f_out = weight.shape
        n_nodes = x.shape[0]
        bu = _tent_basis(edge_attr[:, 0], k1)
        bv = _tent_basis(edge_attr[:, 1], k2)
        basis = (bu[:, :, None] * bv[:, None, :]).reshape(-1, k1 * k2)
        xj = x[edge_index[1]]
        w2 = weight.reshape(k1 * k2, f_in, f_out)
        msg = basis[:, 0:1] * (xj @ w2[0])
        for k in range(1, k1 * k2):
            msg = msg + basis[:, k:k + 1] * (xj @ w2[k])
        out = jax.ops.segment_sum(msg, edge_index[0], num_segments=n_nodes)
        return out

    def _L3_gnn_ref(x, edge_index, pseudo, stn1_w, stn1_b, stn2_w, stn2_b, stn3_w, stn3_b, stn4_w, stn4_b, conv_w, conv_b):
        import jax, jax.numpy as jnp
        import numpy as np
        D = 3
        KS = 5
        K = KS ** D
        S = 2 ** D
        _COMBOS = np.array([[s >> d & 1 for d in range(D)] for s in range(S)], dtype=np.int32)
        _STRIDES = np.array([KS ** (D - 1 - d) for d in range(D)], dtype=np.int32)

        def spline_basis(pseudo):
            pos = pseudo * (KS - 1)
            i0 = jnp.clip(jnp.floor(pos), 0, KS - 2).astype(jnp.int32)
            frac = pos - i0
            combos = jnp.asarray(_COMBOS)
            basis = jnp.prod(jnp.where(combos[None] == 1, frac[:, None, :], 1.0 - frac[:, None, :]), axis=-1)
            idx = jnp.sum((i0[:, None, :] + combos[None]) * jnp.asarray(_STRIDES)[None, None, :], axis=-1)
            return (basis, idx)

        def spline_conv(x, row, col, basis, idx, W, b):
            N = x.shape[0]
            Fout = W.shape[2]
            z = jnp.einsum('ni,kio->nko', x, W).reshape(N * K, Fout)
            gathered = z[col[:, None] * K + idx]
            msg = jnp.einsum('es,eso->eo', basis, gathered)
            out = jax.ops.segment_sum(msg, row, num_segments=N)
            deg = jax.ops.segment_sum(jnp.ones_like(msg[:, 0]), row, num_segments=N)
            return out / jnp.maximum(deg, 1.0)[:, None] + b
        N = x.shape[0]
        row, col = (edge_index[0], edge_index[1])
        basis, idx = spline_basis(pseudo)
        h = jnp.ones((N, 1), x.dtype)
        h = jax.nn.elu(spline_conv(h, row, col, basis, idx, stn1_w, stn1_b))
        h = jax.nn.elu(spline_conv(h, row, col, basis, idx, stn2_w, stn2_b))
        h = jax.nn.elu(h @ stn3_w + stn3_b)
        t = h @ stn4_w + stn4_b
        new_pseudo = jnp.clip(pseudo + t[col] - t[row], 0.0, 1.0)
        basis2, idx2 = spline_basis(new_pseudo)
        return spline_conv(x, row, col, basis2, idx2, conv_w, conv_b)
    edge_index = jnp.stack([src, dst])
    h = jnp.maximum(_layernorm(x, axis=-1), 0.0)
    x = x + _L0_gnn_ref(h, edge_index, L0_gnn_W1a, L0_gnn_b1a, L0_gnn_W2a, L0_gnn_b2a, L0_gnn_W1b, L0_gnn_b1b, L0_gnn_W2b, L0_gnn_b2b)
    h = jnp.maximum(_layernorm(x, axis=-1), 0.0)
    x = x + _L1_gnn_ref(h, edge_attr3_2x32, src, dst, L1_gnn_W1, L1_gnn_b1, L1_gnn_W2s, L1_gnn_b2s, L1_gnn_W2d, L1_gnn_b2d, L1_gnn_attn)
    h = jnp.maximum(_layernorm(x, axis=-1), 0.0)
    x = x + _L2_gnn_ref(h, edge_attr_2, L2_gnn_weight, edge_index)
    h = jnp.maximum(_layernorm(x, axis=-1), 0.0)
    x = x + _L3_gnn_ref(h, edge_index, edge_attr_3, L3_gnn_stn1_w, L3_gnn_stn1_b, L3_gnn_stn2_w, L3_gnn_stn2_b, L3_gnn_stn3_w, L3_gnn_stn3_b, L3_gnn_stn4_w, L3_gnn_stn4_b, L3_gnn_conv_w, L3_gnn_conv_b)
    return x

_drawn_inputs = setup_inputs


def setup_inputs(seed=0):
    import zlib

    import numpy as np

    out = dict(_drawn_inputs(seed))
    spreads = {'L0_gnn_b1a': (0.0, 0.324),
     'L0_gnn_b2a': (0.0, 0.1),
     'L0_gnn_b1b': (0.0, 0.44),
     'L0_gnn_b2b': (0.0, 0.1),
     'L1_gnn_b1': (0.0, 0.1),
     'L1_gnn_b2s': (0.0, 0.8),
     'L1_gnn_b2d': (0.0, 2.0)}
    factors = {'edge_attr3_2x32': 8.0,
     'edge_attr_3': 5.759,
     'L1_gnn_W2s': 8.0,
     'L1_gnn_W2d': 8.0,
     'L1_gnn_attn': 8.0,
     'L3_gnn_stn1_w': 8.0,
     'L3_gnn_stn1_b': 64.0,
     'L3_gnn_stn2_w': 8.0,
     'L3_gnn_stn2_b': 8.0,
     'L3_gnn_stn3_w': 8.0,
     'L3_gnn_stn3_b': 8.0,
     'L3_gnn_stn4_w': 8.0,
     'L3_gnn_stn4_b': 8.0,
     'L3_gnn_conv_w': 5.116,
     'L3_gnn_conv_b': 3.52}
    for name, (base, spread) in spreads.items():
        noise = np.random.default_rng([zlib.crc32(name.encode()), seed]).standard_normal(out[name].shape)
        drawn = base * np.exp(spread * noise) if base else spread * noise
        out[name] = jnp.asarray(drawn.astype(out[name].dtype))
    for name, factor in factors.items():
        out[name] = (out[name] * factor).astype(out[name].dtype)
    return out
```

```python
from contextlib import ExitStack, contextmanager

import concourse.bass as bass
import concourse.mybir as mybir
import numpy as np

F32 = mybir.dt.float32
BF16 = mybir.dt.bfloat16
I32 = mybir.dt.int32
ALU = mybir.AluOpType
ACT = mybir.ActivationFunctionType
AX = mybir.AxisListType

N, E, P = 6250, 100000, 125
NJ, NE = N // P, E // P
LO = 128
HI = -(-N // LO)
BIG = 1.0e30
FAR = 4 * E
D_IN, D_HID, HEADS = 32, 64, 2
K3 = 125


class Phase:

    def __init__(self, nc):
        self.nc, self.made = nc, []

    def sem(self, name):
        s = self.nc.alloc_semaphore(name=f"{name}_{self.nc.next_id()}")
        self.made.append(s)
        return s


@contextmanager
def phase(nc):
    ph = Phase(nc)
    with ExitStack() as ctx:
        ph.ctx = ctx
        yield ph
    nc.clear_and_free_semaphores(ph.made)
    nc.all_engine_barrier()


class Chain:

    def __init__(self, eng, sem):
        self.eng, self.sem, self.base, self.n = eng, sem, 0, 0

    def after(self, ins):
        ins.then_inc(self.sem, 1)
        self.n += 1
        self.eng.wait_ge(self.sem, self.base + self.n)

    def enter(self, i, steps):
        self.start, self.steps = self.base + self.n, steps
        self.base, self.n = self.start + i * steps, 0

    def leave(self, count):
        assert self.n == self.steps, (self.n, self.steps)
        self.base, self.n = self.start + count * self.steps, 0


def sb(k, ph, name, shape, dt=F32):
    ctx = ph.ctx if ph is not None else k.ctx
    return ctx.enter_context(k.nc.sbuf_tensor(f"{name}_{k.nc.next_id()}", shape, dt))


def pb(k, ph, name, shape, dt=F32):
    return ph.ctx.enter_context(k.nc.psum_tensor(f"{name}_{k.nc.next_id()}", shape, dt))


def dram(k, name, shape, dt=F32):
    return k.nc.dram_tensor(f"{name}_{k.nc.next_id()}", shape, dt).ap()


SPLIT = 112


def dma2(eng, out, in_, sem):
    eng.dma_start(out[0:SPLIT], in_[0:SPLIT]).then_inc(sem, 16)
    eng.dma_start(out[SPLIT:P], in_[SPLIT:P]).then_inc(sem, 16)


def edges(ap):
    return ap[0:E].rearrange("(p t) f -> p t f", t=NE)


def nodes(ap):
    return ap[0:N].rearrange("(p j) f -> p j f", j=NJ)


def mid(ap, n):
    return ap.unsqueeze(1).broadcast_to([ap.shape[0], n, ap.shape[1]])


def across(ap, n=128):
    return ap.unsqueeze(0).broadcast_to([n, ap.shape[0]])


def window(ap, offset, dims):
    return bass.AP(ap.tensor, ap.offset + offset, [list(ap.ap[0]), *[list(d) for d in dims]])


def last(ap, n):
    return ap.unsqueeze(len(ap.shape)).broadcast_to([*ap.shape, n])



def constants_phase(k, weights):
    nc = k.nc
    k.column = sb(k, None, "column", [128, 128])
    k.ident = sb(k, None, "ident", [128, 128])
    k.ident16 = sb(k, None, "ident16", [128, 128], BF16)
    k.before = sb(k, None, "before", [128, 128])
    k.ones = sb(k, None, "ones", [128, 128])
    k.column_less = sb(k, None, "column_less", [128, 8])
    k.w = {n: sb(k, None, n, [a.shape[0], int(np.prod(a.shape[1:]))]) for n, a in weights.items()}
    with phase(nc) as ph:
        col_i = sb(k, ph, "col_i", [128, 128], I32)
        diff_i = sb(k, ph, "diff_i", [128, 128], I32)
        diff = sb(k, ph, "diff", [128, 128])
        made, own, loaded = ph.sem("made"), ph.sem("own"), ph.sem("loaded")
        with nc.Block() as block:
            @block.gpsimd
            def _(pool):
                nc.gpsimd.iota(col_i[:], pattern=[[1, 128]], base=0, channel_multiplier=0)
                nc.gpsimd.iota(diff_i[:], pattern=[[1, 128]], base=0, channel_multiplier=-1).then_inc(made, 1)

            @block.sync
            def _(sp):
                for n, a in weights.items():
                    to = k.w[n][:]
                    if len(a.shape) == 3:
                        to = to.rearrange("p (a b) -> p a b", a=a.shape[1])
                    sp.dma_start(to, a).then_inc(loaded, 16)
                sp.wait_ge(loaded, 16 * len(weights))

            @block.vector
            def _(dve):
                c = Chain(dve, own)
                dve.wait_ge(made, 1)
                dve.memset(k.ones[:], 1.0)
                dve.tensor_copy(k.column[:], col_i[:])
                c.after(dve.tensor_copy(diff[:], diff_i[:]))
                dve.tensor_scalar(k.column_less[:], k.column[:, 0:8], -1.0, None, ALU.add)
                dve.tensor_scalar(k.ident[:], diff[:], 0.0, None, ALU.is_equal)
                dve.tensor_scalar(k.ident16[:], diff[:], 0.0, None, ALU.is_equal)
                c.after(dve.tensor_scalar(k.before[:], diff[:], 0.0, None, ALU.is_gt))



GT = 8


def split_keys(dve, c, key_i, hi_i, lo_i, hi, lo):
    c.after(dve.tensor_scalar(hi_i[:], key_i[:], 7, None, ALU.logical_shift_right))
    c.after(dve.tensor_scalar(lo_i[:], key_i[:], LO - 1, None, ALU.bitwise_and))
    dve.tensor_copy(hi[:], hi_i[:])
    c.after(dve.tensor_copy(lo[:], lo_i[:]))


def sort_edges(k, key_dram, width, fill):
    nc = k.nc
    rows = dram(k, "sorted_rows", [E, width])
    first_of, count_of = dram(k, "first_of", [HI, LO]), dram(k, "count_of", [HI, LO])
    with ExitStack() as ctx:
        scope = Scope(ctx)
        hi, lo = sb(k, scope, "hi", [P, NE + GT]), sb(k, scope, "lo", [P, NE + GT])
        row = sb(k, scope, "row", [P, NE, width])
        base = sb(k, scope, "base", [LO, HI])
        count_s = sb(k, scope, "count_s", [LO, HI])
        is_lo = sb(k, scope, "is_lo", [P, 2, GT, LO], BF16)
        is_hi = sb(k, scope, "is_hi", [P, 2, GT, HI], BF16)
        load_keys_phase(k, key_dram, fill, hi, lo, row)
        count_phase(k, hi, lo, is_lo, is_hi, count_s)
        prefix_phase(k, count_s, base, first_of, count_of)
        place_phase(k, hi, lo, is_lo, is_hi, base, row, rows, width)
    return rows, first_of, count_of


class Scope:

    def __init__(self, ctx):
        self.ctx = ctx


def load_keys_phase(k, key_dram, fill, hi, lo, row):
    nc = k.nc
    with phase(nc) as ph:
        key_i, half = sb(k, ph, "key_i", [P, NE], I32), sb(k, ph, "half", [P, 2, NE], I32)
        parts = [sb(k, ph, "part", [P, NE, f], dt) for _, f, dt, _ in fill]
        loaded, numbered, own = ph.sem("loaded"), ph.sem("numbered"), ph.sem("own")
        loads = 1 + sum(src is not None for src, *_ in fill)
        with nc.Block() as block:
            @block.sync
            def _(sp):
                sp.dma_start(key_i[:], key_dram.rearrange("(p t) -> p t", t=NE)).then_inc(loaded, 16)
                for part, (src, f, _, _) in zip(parts, fill):
                    if src is not None:
                        sp.dma_start(part[:], src.rearrange("(p t) f -> p t f", t=NE)).then_inc(loaded, 16)

            @block.gpsimd
            def _(pool):
                for part, (src, *_) in zip(parts, fill):
                    if src is None:
                        nc.gpsimd.iota(part[:, :, 0], pattern=[[1, NE]], base=0,
                                       channel_multiplier=NE).then_inc(numbered, 1)

            @block.vector
            def _(dve):
                c = Chain(dve, own)
                dve.memset(hi[:, NE:], 0.0)
                dve.memset(lo[:, NE:], 0.0)
                c.after(dve.memset(row[:], 0.0))
                dve.wait_ge(loaded, 16 * loads)
                if loads <= len(fill):
                    dve.wait_ge(numbered, 1)
                dve.tensor_scalar(half[:, 0], key_i[:], 7, None, ALU.logical_shift_right)
                c.after(dve.tensor_scalar(half[:, 1], key_i[:], LO - 1, None, ALU.bitwise_and))
                dve.tensor_copy(hi[:, 0:NE], half[:, 0])
                dve.tensor_copy(lo[:, 0:NE], half[:, 1])
                for part, (_, f, _, at) in zip(parts, fill):
                    dve.tensor_copy(row[:, :, at:at + f], part[:])


def one_hots(k, dve, hi, lo, is_hi, is_lo, i, n):
    g, b = (i * 2 + n) * GT, n % 2
    dve.tensor_tensor(is_lo[:, b], mid(k.column[0:P, 0:LO], GT), last(lo[:, bass.ds(g, GT)], LO), ALU.is_equal)
    return dve.tensor_tensor(is_hi[:, b], mid(k.column[0:P, 0:HI], GT), last(hi[:, bass.ds(g, GT)], HI), ALU.is_equal)


def count_phase(k, hi, lo, is_lo, is_hi, count_s):
    nc = k.nc
    with phase(nc) as ph:
        zero16 = sb(k, ph, "zero16", [P, LO], BF16)
        count_p = pb(k, ph, "count_p", [LO, HI])
        zeroed, hot, counted = ph.sem("zeroed"), ph.sem("hot"), ph.sem("counted")
        with nc.Block() as block:
            @block.vector
            def _(dve):
                dve.memset(zero16[:], 0.0).then_inc(zeroed, 1)
                with dve.Fori(0, NE // GT // 2) as i:
                    for b in range(2):
                        dve.wait_ge(counted, i * 2 + b)
                        one_hots(k, dve, hi, lo, is_hi, is_lo, i, b).then_inc(hot, 1)
                dve.wait_ge(counted, NE // GT + 2)
                dve.tensor_copy(count_s[:], count_p[:])

            @block.tensor
            def _(pe):
                pe.wait_ge(zeroed, 1)
                nc.tensor.matmul(count_p[:], zero16[:], zero16[:, 0:HI], start=True, stop=False).then_inc(counted, 1)
                with pe.Fori(0, NE // GT // 2) as i:
                    for b in range(2):
                        pe.wait_ge(hot, i * 2 + b + 1)
                        for t in range(GT):
                            m = nc.tensor.matmul(count_p[:], is_lo[:, b, t, :], is_hi[:, b, t, :],
                                                 start=False, stop=False)
                        m.then_inc(counted, 1)
                nc.tensor.matmul(count_p[:], zero16[:], zero16[:, 0:HI], start=False, stop=True).then_inc(counted, 1)


def prefix_phase(k, count_s, base, first_of, count_of):
    nc = k.nc
    with phase(nc) as ph:
        below_p, total_p = pb(k, ph, "below_p", [LO, HI]), pb(k, ph, "total_p", [LO, HI])
        turned_p = pb(k, ph, "turned_p", [HI, 2, LO])
        total_s, upto = sb(k, ph, "total_s", [LO, HI]), sb(k, ph, "upto", [LO, HI])
        turned = sb(k, ph, "turned", [HI, 2, LO])
        summed, own, turns, copied, stored = (ph.sem(n) for n in ("summed", "own", "turns", "copied", "stored"))
        with nc.Block() as block:
            @block.tensor
            def _(pe):
                nc.tensor.matmul(below_p[:], k.before[:], count_s[:], start=True, stop=True)
                nc.tensor.matmul(total_p[:], k.ones[:], count_s[:], start=True, stop=True).then_inc(summed, 1)
                pe.wait_ge(own, 4)
                nc.tensor.transpose(turned_p[:, 0, :], base[:], k.ident[:])
                nc.tensor.transpose(turned_p[:, 1, :], count_s[:], k.ident[:]).then_inc(turns, 1)

            @block.vector
            def _(dve):
                c = Chain(dve, own)
                dve.wait_ge(summed, 1)
                c.after(dve.tensor_copy(total_s[:], total_p[:]))
                c.after(dve.tensor_tensor_scan(out=upto[:], data0=k.ones[:, 0:HI], data1=total_s[:], initial=0.0,
                                               op0=ALU.mult, op1=ALU.add))
                c.after(dve.tensor_tensor(upto[:], upto[:], total_s[:], ALU.subtract))
                c.after(dve.tensor_tensor(base[:], upto[:], below_p[:], ALU.add))
                dve.wait_ge(turns, 1)
                dve.tensor_copy(turned[:], turned_p[:]).then_inc(copied, 1)

            @block.sync
            def _(sp):
                sp.wait_ge(copied, 1)
                sp.dma_start(first_of, turned[:, 0, :]).then_inc(stored, 16)
                sp.dma_start(count_of, turned[:, 1, :]).then_inc(stored, 16)
                sp.wait_ge(stored, 32)


def place_phase(k, hi, lo, is_lo, is_hi, base, row, rows, width):
    nc = k.nc
    half = GT // 2
    pairs = NE // GT // 2
    with phase(nc) as ph:
        turned_p = pb(k, ph, "turned_p", [LO, GT, 128], BF16)
        match_p = [pb(k, ph, f"match_p{b}", [P, half, P]) for b in range(2)]
        rank_p = [pb(k, ph, f"rank_p{b}", [P, GT, HI]) for b in range(2)]
        next_p = pb(k, ph, "next_p", [LO, GT + 1, HI])
        lo_t = sb(k, ph, "lo_t", [LO, GT, P])
        lo_t16 = sb(k, ph, "lo_t16", [LO, GT, P], BF16)
        earlier = sb(k, ph, "earlier", [P, 2, half, P], BF16)
        next_s = [sb(k, ph, "next_s", [LO, GT + 1, HI]) for _ in range(2)]
        picked, pos = sb(k, ph, "picked", [P, GT, HI]), sb(k, ph, "pos", [P, GT])
        pos_i = [sb(k, ph, "pos_i", [P, GT], I32) for _ in range(2)]
        row_now = [sb(k, ph, "row_now", [P, GT, width]) for _ in range(2)]
        names = ("hot", "turned", "copied", "matched", "masked", "begun", "moved", "snapped", "ranked", "own", "placed", "seen")
        hot, turned, copied, matched, masked, begun, moved, snapped, ranked, own, placed, seen = (ph.sem(n) for n in names)
        scattered = [ph.sem("scattered0"), ph.sem("scattered1")]
        with nc.Block() as block:
            @block.vector
            def _(dve):
                c = Chain(dve, own)
                dve.tensor_copy(next_s[1][:, GT, :], base[:]).then_inc(begun, 1)
                one_hots(k, dve, hi, lo, is_hi, is_lo, 0, 0).then_inc(hot, 1)
                with dve.Fori(0, pairs) as i:
                    c.enter(i, 4)
                    for b in range(2):
                        g = i * 2 + b
                        dve.wait_ge(ranked, g)
                        one_hots(k, dve, hi, lo, is_hi, is_lo, i, b + 1).then_inc(hot, 1)
                        for h in range(2):
                            dve.wait_ge(matched, g * 2 + h + 1)
                            dve.tensor_tensor(earlier[:, h], match_p[h][:], mid(k.before[0:P, 0:P], half),
                                              ALU.mult).then_inc(masked, 1)
                        dve.wait_ge(ranked, g + 1)
                        c.after(dve.tensor_tensor(picked[:], rank_p[b][:], is_hi[:, b], ALU.mult))
                        c.after(dve.tensor_reduce(pos[:], picked[:], AX.X, ALU.add))
                        dve.wait_ge(scattered[b], i * (16 * GT))
                        dve.tensor_copy(pos_i[b][:], pos[:])
                        dve.tensor_copy(row_now[b][:], row[:, bass.ds(g * GT, GT), :]).then_inc(placed, 1)
                    c.leave(pairs)

            @block.scalar
            def _(act):
                with act.Fori(0, pairs) as i:
                    for b in range(2):
                        g = i * 2 + b
                        act.wait_ge(turned, g + 1)
                        act.wait_ge(ranked, g)
                        nc.scalar.copy(lo_t16[:], turned_p[:, :, 0:P]).then_inc(copied, 1)
                        nc.scalar.copy(lo_t[:], turned_p[:, :, 0:P]).then_inc(copied, 1)
                        act.wait_ge(moved, g + 1)
                        nc.scalar.copy(next_s[b][:], next_p[:]).then_inc(snapped, 1)

            @block.tensor
            def _(pe):
                pe.wait_ge(begun, 1)
                with pe.Fori(0, pairs) as i:
                    for b in range(2):
                        g = i * 2 + b
                        pe.wait_ge(hot, g + 1)
                        pe.wait_ge(copied, g * 2)
                        for t in range(GT):
                            m = nc.tensor.transpose(turned_p[:, t, 0:P], is_lo[:, b, t, :], k.ident16[0:P, 0:P])
                        m.then_inc(turned, 1)
                        pe.wait_ge(snapped, g)
                        for t in range(GT + 1):
                            m = nc.tensor.matmul(next_p[:, t, :], k.ident[:], next_s[1 - b][:, GT, :], start=True, stop=t == 0)
                            for u in range(t):
                                m = nc.tensor.matmul(next_p[:, t, :], is_lo[:, b, u, :], is_hi[:, b, u, :],
                                                     start=False, stop=u == t - 1)
                        m.then_inc(moved, 1)
                        pe.wait_ge(copied, g * 2 + 1)
                        pe.wait_ge(masked, g * 2)
                        for h in range(2):
                            for t in range(half):
                                one = lo_t16[:, h * half + t, :]
                                m = nc.tensor.matmul(match_p[h][:, t, :], one, one, start=True, stop=True)
                            m.then_inc(matched, 1)
                        pe.wait_ge(copied, g * 2 + 2)
                        pe.wait_ge(masked, g * 2 + 2)
                        pe.wait_ge(snapped, g + 1)
                        for t in range(GT):
                            nc.tensor.matmul(rank_p[b][:, t, :], lo_t[:, t, :], next_s[b][:, t, :], start=True, stop=False)
                            m = nc.tensor.matmul(rank_p[b][:, t, :], earlier[:, t // half, t % half, :],
                                                 is_hi[:, b, t, :], start=False, stop=True)
                        m.then_inc(ranked, 1)

            @block.gpsimd
            def _(pool):
                with pool.Fori(0, pairs) as i:
                    for b in range(2):
                        pool.wait_ge(placed, i * 2 + b + 1)
                        pool.sem_inc(seen, 1)
                        for t in range(GT):
                            pool.indirect_dma_start(
                                out=rows, out_offset=bass.IndirectOffsetOnAxis(ap=pos_i[b][:, t:t + 1], axis=0),
                                in_=row_now[b][:, t, :], in_offset=None).then_inc(scattered[b], 16)
                for b in range(2):
                    pool.wait_ge(scattered[b], pairs * 16 * GT)



class Order:
    pass


def make_order(k, rows, first_of, count_of, width, take):
    nc, o = k.nc, Order()
    o.same = sb(k, None, "same", [P, NE])
    o.carry = sb(k, None, "carry", [64 * 2, P])
    o.end = sb(k, None, "end", [P, NJ], I32)
    o.crossed = sb(k, None, "crossed", [P, NJ], I32)
    o.first = sb(k, None, "first", [P, NJ], I32)
    o.degree = sb(k, None, "degree", [P, NJ])
    o.head = sb(k, None, "head", [P, 1], I32)
    o.kept = [sb(k, None, "kept", [P, NE, f], dt) for _, f, dt in take]
    carry_d = dram(k, "carry", [P, 1])
    with phase(nc) as ph:
        row = sb(k, ph, "row", [P, NE, width])
        key = sb(k, ph, "key", [P, NE + 1])
        pass_on = sb(k, ph, "pass_on", [P, 1])
        first, t1, t2, some = (sb(k, ph, n, [P, NJ]) for n in ("first", "t1", "t2", "some"))
        q_i = sb(k, ph, "q_i", [P, NJ], I32)
        loaded, own, ready, stored, spread = (ph.sem(n) for n in ("loaded", "own", "ready", "stored", "spread"))
        with nc.Block() as block:
            @block.sync
            def _(sp):
                dma2(sp, row[:], edges(rows), loaded)
                sp.dma_start(first[:], first_of.rearrange("h l -> (h l)")[0:N].rearrange("(p j) -> p j", j=NJ)).then_inc(loaded, 16)
                sp.dma_start(o.degree[:], count_of.rearrange("h l -> (h l)")[0:N].rearrange("(p j) -> p j", j=NJ)).then_inc(loaded, 16)
                sp.wait_ge(ready, 1)
                sp.dma_start(key[1:P, 0:1], edges(rows)[0:P - 1, NE - 1, 0:1],
                             allow_slow_non_contiguous=True).then_inc(loaded, 16)
                sp.wait_ge(ready, 2)
                sp.dma_start(carry_d, pass_on[:]).then_inc(stored, 16)
                sp.wait_ge(stored, 16)
                sp.dma_start(o.carry[:], across(carry_d.rearrange("p f -> (p f)"))).then_inc(spread, 16)
                sp.wait_ge(spread, 16)

            @block.vector
            def _(dve):
                c = Chain(dve, own)
                dve.memset(key[:, 0:1], -1.0).then_inc(ready, 1)
                dve.wait_ge(loaded, 80)
                c.after(dve.tensor_copy(key[:, 1:], row[:, :, 0]))
                dve.tensor_copy(o.head[:], key[:, 1:2])
                c.after(dve.tensor_tensor(o.same[:], key[:, 1:], key[:, 0:NE], ALU.is_equal))
                c.after(dve.tensor_tensor(pass_on[:], key[:, 1:2], key[:, NE:NE + 1], ALU.is_equal))
                dve.tensor_tensor(pass_on[:], pass_on[:], o.same[:, 0:1], ALU.mult).then_inc(ready, 1)
                for kept, (at, f, _) in zip(o.kept, take):
                    dve.tensor_copy(kept[:], row[:, :, at:at + f])
                c.after(dve.tensor_scalar(some[:], o.degree[:], 0.0, None, ALU.is_gt))
                c.after(dve.tensor_scalar(t1[:], some[:], -float(FAR), float(FAR), ALU.mult, ALU.add))
                c.after(dve.tensor_tensor(o.first[:], t1[:], first[:], ALU.add))
                c.after(dve.tensor_tensor(t1[:], first[:], o.degree[:], ALU.add))
                c.after(dve.tensor_scalar(t1[:], t1[:], -float(E + 1), None, ALU.add))
                c.after(dve.tensor_tensor(t1[:], t1[:], some[:], ALU.mult))
                c.after(dve.tensor_scalar(t1[:], t1[:], float(E), None, ALU.add))
                c.after(dve.tensor_copy(o.end[:], t1[:]))
                c.after(dve.tensor_scalar(t2[:], t1[:], 0.5, 1.0 / NE, ALU.add, ALU.mult))
                c.after(dve.tensor_copy(q_i[:], t2[:]))
                c.after(dve.tensor_copy(t2[:], q_i[:]))
                c.after(dve.tensor_scalar(t2[:], t2[:], float(NE), None, ALU.mult))
                c.after(dve.tensor_tensor(t1[:], t2[:], t1[:], ALU.is_gt))
                c.after(dve.scalar_tensor_tensor(t2[:], t1[:], -float(NE), t2[:], ALU.mult, ALU.add))
                c.after(dve.tensor_tensor(t1[:], first[:], t2[:], ALU.is_lt))
                c.after(dve.tensor_tensor(t1[:], t1[:], some[:], ALU.mult))
                c.after(dve.tensor_scalar(t2[:], t2[:], 1.0 / NE, None, ALU.mult))
                c.after(dve.tensor_tensor(t2[:], t2[:], t1[:], ALU.mult))
                c.after(dve.tensor_copy(o.crossed[:], t2[:]))
    return o



def edge_pass(k, o, T, tables, streams, F, work, steps, out=None, keep=None, extra=(), exp_of=None):
    nc = k.nc
    pairs = NE // T // 2
    state = sb(k, None, "state", [P, max(F, 1)]) if F else None
    with phase(nc) as ph:
        got = [[sb(k, ph, "got", [P, T, w]) for _ in range(2)] for _, _, w in tables]
        read = [[sb(k, ph, "read", [P, T, w]) for _ in range(2)] for _, w in streams]
        res = [sb(k, ph, "res", [P, T, F]) for _ in range(2)] if F else None
        idx = [[sb(k, ph, "idx", [P, T], I32) for _ in range(2)] for _ in tables]
        tmp = [sb(k, ph, "tmp", [P, T, *shape]) for shape in extra]
        indexed, seen, own, done, exped = (ph.sem(n) for n in ("indexed", "seen", "own", "done", "exped"))
        gathered, loaded, stored, used = ([ph.sem(f"{n}{b}") for b in range(2)] for n in ("gathered", "loaded", "stored", "used"))
        to_exp = ph.sem("to_exp")
        stores = 32 * (bool(out is not None) + bool(keep))
        with nc.Block() as block:
            if tables:
                @block.gpsimd
                def _(pool):
                    with pool.Fori(0, pairs) as i:
                        for b in range(2):
                            g = i * 2 + b
                            pool.wait_ge(used[b], i)
                            if keep:
                                pool.wait_ge(stored[b], i * stores)
                            for n, (_, index, _) in enumerate(tables):
                                pool.tensor_copy(idx[n][b][:], index(bass.ds(g * T, T))).then_inc(indexed, 1)
                            pool.wait_ge(indexed, (g + 1) * len(tables))
                            pool.sem_inc(seen, 1)
                            for n, (table, _, _) in enumerate(tables):
                                for t in range(T):
                                    pool.indirect_dma_start(
                                        out=got[n][b][:, t, :], out_offset=None, in_=table,
                                        in_offset=bass.IndirectOffsetOnAxis(ap=idx[n][b][:, t:t + 1], axis=0)
                                    ).then_inc(gathered[b], 16)

            if streams:
                @block.sync
                def _(sp):
                    with sp.Fori(0, pairs) as i:
                        for b in range(2):
                            sp.wait_ge(used[b], i)
                            for n, (rows, _) in enumerate(streams):
                                dma2(sp, read[n][b][:], edges(rows)[:, bass.ds((i * 2 + b) * T, T), :], loaded[b])

            @block.vector
            def _(dve):
                c = Chain(dve, own)
                if F:
                    c.after(dve.memset(state[:], 0.0))
                with dve.Fori(0, pairs) as i:
                    c.enter(i, 2 * (steps + (2 if F else 0)))
                    for b in range(2):
                        if tables:
                            dve.wait_ge(gathered[b], (i + 1) * (16 * T * len(tables)))
                        if streams:
                            dve.wait_ge(loaded[b], (i + 1) * (32 * len(streams)))
                        if out is not None:
                            dve.wait_ge(stored[b], i * stores)
                        at = bass.ds((i * 2 + b) * T, T)
                        src = work(dve, c, at, [x[b] for x in got], [x[b] for x in read], tmp,
                                   res[b] if F else None, (to_exp, exped, i * 2 + b + 1))
                        if F:
                            for f in range(F):
                                m = dve.tensor_tensor_scan(out=res[b][:, :, f], data0=o.same[:, at], data1=src[:, :, f],
                                                           initial=state[:, f:f + 1], op0=ALU.mult, op1=ALU.add)
                            c.after(m)
                            dve.tensor_copy(state[:], res[b][:, T - 1, :]).then_inc(own, 1)
                            c.n += 1
                            dve.wait_ge(own, c.base + c.n)
                        dve.sem_inc(used[b], 1)
                        dve.sem_inc(done, 1)
                    c.leave(pairs)

            @block.scalar
            def _(act):
                if exp_of is None and not stores:
                    return
                with act.Fori(0, pairs) as i:
                    for b in range(2):
                        g = i * 2 + b
                        if exp_of is not None:
                            act.wait_ge(to_exp, g + 1)
                            nc.scalar.activation(tmp[exp_of][:], tmp[exp_of][:], ACT.Exp).then_inc(exped, 1)
                        if keep:
                            act.wait_ge(gathered[b], (i + 1) * (16 * T * len(tables)))
                            dma2(act, edges(keep[1])[:, bass.ds(g * T, T), :], got[keep[0]][b][:], stored[b])
                        if out is not None:
                            act.wait_ge(done, g + 1)
                            dma2(act, edges(out)[:, bass.ds(g * T, T), :], res[b][:], stored[b])
                if stores:
                    for b in range(2):
                        act.wait_ge(stored[b], pairs * stores)
    return state


def carry_phase(k, o, state, F, rows, op=ALU.add, zero=0.0):
    nc = k.nc
    table = dram(k, "carried", [P + 1, F])
    with phase(nc) as ph:
        state_p = pb(k, ph, "state_p", [F, P])
        back_p = pb(k, ph, "back_p", [P, F])
        state_t, total_t = sb(k, ph, "state_t", [F, P]), sb(k, ph, "total_t", [F, P])
        flags = sb(k, ph, "flags", [F, P])
        total, nothing = sb(k, ph, "total", [P, F]), sb(k, ph, "nothing", [1, F])
        own, turned, back, ready, stored = (ph.sem(n) for n in ("own", "turned", "back", "ready", "stored"))
        with nc.Block() as block:
            @block.tensor
            def _(pe):
                nc.tensor.transpose(state_p[:], state[:], k.ident[0:P, 0:P]).then_inc(turned, 1)
                pe.wait_ge(own, 4)
                nc.tensor.transpose(back_p[:], total_t[:], k.ident[0:F, 0:F]).then_inc(back, 1)

            @block.vector
            def _(dve):
                c = Chain(dve, own)
                c.after(dve.memset(nothing[:], zero))
                if op == ALU.max:
                    c.after(dve.tensor_scalar(flags[:], o.carry[0:F, :], BIG, -BIG, ALU.mult, ALU.add))
                else:
                    c.after(dve.tensor_copy(flags[:], o.carry[0:F, :]))
                dve.wait_ge(turned, 1)
                c.after(dve.tensor_copy(state_t[:], state_p[:]))
                c.after(dve.tensor_tensor_scan(out=total_t[:], data0=flags[:], data1=state_t[:], initial=zero,
                                               op0=ALU.add if op == ALU.max else ALU.mult, op1=op))
                dve.wait_ge(back, 1)
                dve.tensor_copy(total[:], back_p[:]).then_inc(ready, 1)

            @block.sync
            def _(sp):
                sp.wait_ge(own, 1)
                sp.dma_start(table[0:1, :], nothing[:]).then_inc(stored, 16)
                sp.dma_start(rows[E:E + 1, :], nothing[:]).then_inc(stored, 16)
                sp.wait_ge(ready, 1)
                sp.dma_start(table[1:P + 1, :], total[:]).then_inc(stored, 16)
                sp.wait_ge(stored, 48)
    return table


def collect_phase(k, o, rows, table, F, dest, op=ALU.add):
    nc = k.nc
    with phase(nc) as ph:
        carried = sb(k, ph, "carried", [P, NJ, F])
        gathered, own = ph.sem("gathered"), ph.sem("own")
        with nc.Block() as block:
            @block.gpsimd
            def _(pool):
                for dst, src, index in ((dest, rows, o.end), (carried, table, o.crossed)):
                    for j in range(NJ):
                        pool.indirect_dma_start(
                            out=dst[:, j, :], out_offset=None, in_=src,
                            in_offset=bass.IndirectOffsetOnAxis(ap=index[:, j:j + 1], axis=0)).then_inc(gathered, 16)

            @block.vector
            def _(dve):
                dve.wait_ge(gathered, 32 * NJ)
                dve.tensor_tensor(dest[:], dest[:], carried[:], op).then_inc(own, 1)


def scatter_nodes_phase(k, o, src, F):
    nc = k.nc
    spread, table = dram(k, "spread", [E, F]), dram(k, "node_rows", [N, F])
    head = sb(k, None, "head_row", [P, F])
    cols = 3200 // F if F in (32, 64) else 800
    with phase(nc) as ph:
        zeros = sb(k, ph, "zeros", [P, cols, F])
        zeroed = ph.sem("zeroed")
        cleared, stored, scattered = ph.sem("cleared"), ph.sem("stored"), ph.sem("scattered")
        pieces = NE // cols
        with nc.Block() as block:
            @block.vector
            def _(dve):
                dve.memset(zeros[:], 0.0).then_inc(zeroed, 1)

            @block.sync
            def _(sp):
                sp.wait_ge(zeroed, 1)
                for n in range(pieces):
                    dma2(sp, edges(spread)[:, n * cols:(n + 1) * cols, :], zeros[:], cleared)

            @block.scalar
            def _(act):
                act.dma_start(nodes(table), src[:]).then_inc(stored, 16)
                act.wait_ge(stored, 16)

            @block.gpsimd
            def _(pool):
                pool.wait_ge(cleared, 32 * pieces)
                for j in range(NJ):
                    pool.indirect_dma_start(
                        out=spread, out_offset=bass.IndirectOffsetOnAxis(ap=o.first[:, j:j + 1], axis=0),
                        in_=src[:, j, :], in_offset=None, bounds_check=E - 1, oob_is_err=False).then_inc(scattered, 16)
                pool.wait_ge(stored, 16)
                pool.indirect_dma_start(out=head[:], out_offset=None, in_=table,
                                        in_offset=bass.IndirectOffsetOnAxis(ap=o.head[:], axis=0)).then_inc(scattered, 16)
                pool.wait_ge(scattered, 16 * (NJ + 1))
    return spread, head, table


def store_nodes_phase(k, src, F):
    nc = k.nc
    table = dram(k, "node_rows", [N, F])
    with phase(nc) as ph:
        stored = ph.sem("stored")
        with nc.Block() as block:
            @block.sync
            def _(sp):
                sp.dma_start(nodes(table), src[:]).then_inc(stored, 16)
                sp.wait_ge(stored, 16)
    return table



JG = 5


def dense_phase(k, src, K, weight, C, dest, bias=None, relu=False):
    nc = k.nc
    pairs = NJ // JG // 2
    with phase(nc) as ph:
        now = [sb(k, ph, "now", [P, JG, K]) for _ in range(2)]
        turned = [sb(k, ph, "turned", [K, JG, P]) for _ in range(2)]
        turned_p = [pb(k, ph, f"turned_p{b}", [K, JG, 128]) for b in range(2)]
        made_p = [pb(k, ph, f"made_p{b}", [P, JG, C]) for b in range(2)]
        taken, seen, flipped, copied, made, out = (ph.sem(n) for n in ("taken", "seen", "flipped", "copied", "made", "out"))
        with nc.Block() as block:
            @block.vector
            def _(dve):
                with dve.Fori(0, pairs) as i:
                    for b in range(2):
                        g = i * 2 + b
                        dve.wait_ge(copied, i * 2)
                        dve.tensor_copy(now[b][:], src[:, bass.ds(g * JG, JG), :]).then_inc(taken, 1)
                        dve.wait_ge(made, g + 1)
                        o = dest[:, bass.ds(g * JG, JG), :]
                        if relu:
                            dve.tensor_scalar(o, made_p[b][:], 0.0, None, ALU.max).then_inc(out, 1)
                        else:
                            dve.tensor_copy(o, made_p[b][:]).then_inc(out, 1)

            @block.tensor
            def _(pe):
                with pe.Fori(0, pairs) as i:
                    for b in range(2):
                        g = i * 2 + b
                        pe.wait_ge(taken, g + 1)
                        pe.sem_inc(seen, 1)
                        for j in range(JG):
                            m = nc.tensor.transpose(turned_p[b][:, j, 0:P], now[b][:, j, :], k.ident[0:P, 0:P])
                        m.then_inc(flipped, 1)
                        pe.wait_ge(copied, g + 1)
                        pe.wait_ge(out, i * 2)
                        for j in range(JG):
                            m = nc.tensor.matmul(made_p[b][:, j, :], turned[b][:, j, :], weight, start=True, stop=bias is None)
                            if bias is not None:
                                m = nc.tensor.matmul(made_p[b][:, j, :], k.ones[0:1, 0:P], bias, start=False, stop=True)
                        m.then_inc(made, 1)

            @block.scalar
            def _(act):
                with act.Fori(0, pairs) as i:
                    for b in range(2):
                        act.wait_ge(flipped, i * 2 + b + 1)
                        nc.scalar.copy(turned[b][:], turned_p[b][:, :, 0:P]).then_inc(copied, 1)


def norm_phase(k, x, dest):
    nc = k.nc
    with phase(nc) as ph:
        mean, var, root = (sb(k, ph, n, [P, NJ]) for n in ("mean", "var", "root"))
        cent, sq = sb(k, ph, "cent", [P, NJ, D_IN]), sb(k, ph, "sq", [P, NJ, D_IN])
        own, ready, rooted = ph.sem("own"), ph.sem("ready"), ph.sem("rooted")
        with nc.Block() as block:
            @block.vector
            def _(dve):
                c = Chain(dve, own)
                c.after(dve.tensor_reduce(mean[:], x[:], AX.X, ALU.add))
                c.after(dve.tensor_scalar(mean[:], mean[:], 1.0 / D_IN, None, ALU.mult))
                c.after(dve.tensor_tensor(cent[:], x[:], last(mean[:], D_IN), ALU.subtract))
                c.after(dve.tensor_tensor(sq[:], cent[:], cent[:], ALU.mult))
                c.after(dve.tensor_reduce(var[:], sq[:], AX.X, ALU.add))
                dve.tensor_scalar(var[:], var[:], 1.0 / D_IN, 1e-5, ALU.mult, ALU.add).then_inc(ready, 1)
                dve.wait_ge(rooted, 1)
                c.after(dve.reciprocal(root[:], root[:]))
                c.after(dve.tensor_tensor(cent[:], cent[:], last(root[:], D_IN), ALU.mult))
                dve.tensor_scalar(dest[:], cent[:], 0.0, None, ALU.max)

            @block.scalar
            def _(act):
                act.wait_ge(ready, 1)
                nc.scalar.activation(root[:], var[:], ACT.Sqrt).then_inc(rooted, 1)


def load_phase(k, dest, src):
    with phase(k.nc) as ph:
        loaded = ph.sem("loaded")
        with k.nc.Block() as block:
            @block.sync
            def _(sp):
                sp.dma_start(dest, src).then_inc(loaded, 16)
                sp.wait_ge(loaded, 16)


def dve_phase(k, body):
    nc = k.nc
    with phase(nc) as ph:
        own = ph.sem("own")
        with nc.Block() as block:
            @block.vector
            def _(dve):
                body(dve, Chain(dve, own), ph)


def elu_phase(k, v, C, bias=None, degree=None):
    nc = k.nc
    with phase(nc) as ph:
        low, d = sb(k, ph, "low", [P, NJ, C]), sb(k, ph, "d", [P, NJ])
        own, ready, exped = ph.sem("own"), ph.sem("ready"), ph.sem("exped")
        with nc.Block() as block:
            @block.vector
            def _(dve):
                c = Chain(dve, own)
                mean_and_bias(dve, c, v, C, bias, degree, d)
                dve.tensor_scalar(low[:], v[:], 0.0, None, ALU.min).then_inc(ready, 1)
                dve.wait_ge(exped, 1)
                c.after(dve.tensor_scalar(v[:], v[:], 0.0, -1.0, ALU.max, ALU.add))
                dve.tensor_tensor(v[:], v[:], low[:], ALU.add)

            @block.scalar
            def _(act):
                act.wait_ge(ready, 1)
                nc.scalar.activation(low[:], low[:], ACT.Exp).then_inc(exped, 1)


def mean_and_bias(dve, c, v, C, bias, degree, d):
    if degree is not None:
        c.after(dve.tensor_scalar(d[:], degree[:], 1.0, None, ALU.max))
        c.after(dve.reciprocal(d[:], d[:]))
        c.after(dve.tensor_tensor(v[:], v[:], last(d[:], C), ALU.mult))
    if bias is not None:
        c.after(dve.tensor_tensor(v[:], v[:], mid(bias, NJ), ALU.add))


def table_phase(k, src, K, weight, C, rows, side, paired, table):
    nc = k.nc
    cells = side - 1
    floats = cells * rows * 2 * C if paired else rows * side * C
    if paired:
        most = 512 // (side * C)
        sizes = [min(most, rows - r) * side * C for r in range(0, rows, most)]
    else:
        sizes = [500] * (floats // 500)
    starts = [sum(sizes[:q]) for q in range(len(sizes))]
    parts, banks = len(sizes), 6
    flat = nodes(table.rearrange("(n c) f -> n (c f)", n=N))
    with phase(nc) as ph:
        now = [sb(k, ph, "now", [P, K]) for _ in range(2)]
        turned = [sb(k, ph, "turned", [K, P]) for _ in range(2)]
        z = [sb(k, ph, "z", [P, floats]) for _ in range(2)]
        turned_p = pb(k, ph, "turned_p", [K, 128])
        made_p = [pb(k, ph, f"made_p{n}", [P, 512]) for n in range(banks)]
        taken, seen, ready, flipped, copied, made = (
            ph.sem(n) for n in ("taken", "seen", "ready", "flipped", "copied", "made"))
        stored = [ph.sem("stored0"), ph.sem("stored1")]
        out = [ph.sem("out0"), ph.sem("out1")]
        mine = [[q for q in range(parts) if q % 2 == e] for e in range(2)]
        per = [len(m) for m in mine]
        stores = 32

        with nc.Block() as block:
            def evacuate(eng, e, i, b, copy):
                g = i * 2 + b
                eng.wait_ge(stored[b], i * stores)
                for q in mine[e]:
                    eng.wait_ge(made, g * parts + q + 1)
                    if paired:
                        r, n = starts[q] // (side * C), sizes[q] // (side * C)
                        to = window(z[b][:], r * 2 * C, [(rows * 2 * C, cells), (2 * C, n), (1, 2 * C)])
                        of = window(made_p[q % banks][:], 0, [(C, cells), (side * C, n), (1, 2 * C)])
                    else:
                        to, of = z[b][:, starts[q]:starts[q] + sizes[q]], made_p[q % banks][:, 0:sizes[q]]
                    copy(to, of).then_inc(out[e], 1)

            @block.vector
            def _(dve):
                with dve.Fori(0, NJ // 2) as i:
                    for b in range(2):
                        g = i * 2 + b
                        dve.wait_ge(flipped, g)
                        dve.tensor_copy(now[b][:], src[:, bass.ds(g, 1), :].rearrange("p a k -> p (a k)")).then_inc(taken, 1)
                        dve.wait_ge(flipped, g + 1)
                        dve.tensor_copy(turned[b][:], turned_p[:, 0:P]).then_inc(copied, 1)
                        evacuate(dve, 0, i, b, dve.tensor_copy)

            @block.scalar
            def _(act):
                if mine[1]:
                    with act.Fori(0, NJ // 2) as i:
                        for b in range(2):
                            evacuate(act, 1, i, b, nc.scalar.copy)

            @block.tensor
            def _(pe):
                with pe.Fori(0, NJ // 2) as i:
                    for b in range(2):
                        g = i * 2 + b
                        pe.wait_ge(taken, g + 1)
                        pe.sem_inc(seen, 1)
                        nc.tensor.transpose(turned_p[:, 0:P], now[b][:], k.ident[0:P, 0:P]).then_inc(flipped, 1)
                        pe.wait_ge(copied, g + 1)
                        for q in range(parts):
                            if q < 2 and mine[q]:
                                pe.wait_ge(out[q], g * per[q])
                            if q >= banks:
                                e = (q - banks) % 2
                                pe.wait_ge(out[e], g * per[e] + mine[e].index(q - banks) + 1)
                            nc.tensor.matmul(made_p[q % banks][:, 0:sizes[q]], turned[b][:],
                                             weight[:, starts[q]:starts[q] + sizes[q]],
                                             start=True, stop=True).then_inc(made, 1)

            @block.sync
            def _(sp):
                with sp.Fori(0, NJ // 2) as i:
                    for b in range(2):
                        g = i * 2 + b
                        for e in range(2):
                            if mine[e]:
                                sp.wait_ge(out[e], (g + 1) * per[e])
                                sp.sem_inc(ready, 1)
                        dma2(sp, flat[:, bass.ds(g, 1), :].rearrange("p a f -> p (a f)"), z[b][:], stored[b])
                for slot in stored:
                    sp.wait_ge(slot, NJ // 2 * stores)



def segment_phase(k, o, v, F, op):
    nc = k.nc
    zero = -BIG if op == ALU.max else 0.0
    rows = dram(k, "rows", [E + 1, F])
    state = sb(k, None, "state", [P, F])
    dest = sb(k, None, "segment", [P, NJ, F])
    with phase(nc) as ph:
        run, flags = sb(k, ph, "run", [P, NE, F]), sb(k, ph, "flags", [P, NE])
        own, done, stored = ph.sem("own"), ph.sem("done"), ph.sem("stored")
        with nc.Block() as block:
            @block.vector
            def _(dve):
                c = Chain(dve, own)
                if op == ALU.max:
                    c.after(dve.tensor_scalar(flags[:], o.same[:], BIG, -BIG, ALU.mult, ALU.add))
                else:
                    c.after(dve.tensor_copy(flags[:], o.same[:]))
                for f in range(F):
                    m = dve.tensor_tensor_scan(out=run[:, :, f], data0=flags[:], data1=v[:, :, f], initial=zero,
                                               op0=ALU.add if op == ALU.max else ALU.mult, op1=op)
                c.after(m)
                dve.tensor_copy(state[:], run[:, NE - 1, :]).then_inc(done, 1)

            @block.sync
            def _(sp):
                sp.wait_ge(done, 1)
                dma2(sp, edges(rows), run[:], stored)
                sp.wait_ge(stored, 32)
    table = carry_phase(k, o, state, F, rows, op, zero)
    collect_phase(k, o, rows, table, F, dest, op)
    return dest


def expand_phase(k, o, src, F, dest):
    nc = k.nc
    spread, head, _ = scatter_nodes_phase(k, o, src, F)
    with phase(nc) as ph:
        loaded, own = ph.sem("loaded"), ph.sem("own")
        first = sb(k, ph, "first", [P, NE, F])
        with nc.Block() as block:
            @block.sync
            def _(sp):
                dma2(sp, first[:], edges(spread), loaded)

            @block.vector
            def _(dve):
                dve.wait_ge(loaded, 32)
                for f in range(F):
                    dve.tensor_tensor_scan(out=dest[:, :, f], data0=o.same[:], data1=first[:, :, f],
                                           initial=head[:, f:f + 1], op0=ALU.mult, op1=ALU.add)


@contextmanager
def layer(k):
    outer = k.ctx
    with ExitStack() as ctx:
        k.ctx = ctx
        yield
    k.ctx = outer


def add_phase(k, dest, other):
    def body(dve, c, ph):
        dve.tensor_tensor(dest[:], dest[:], other[:], ALU.add)
    dve_phase(k, body)


def aggregate(k, o, table, index, F, dest):
    rows = dram(k, "rows", [E + 1, F])

    def work(dve, c, at, got, read, tmp, res, exp):
        return got[0]
    state = edge_pass(k, o, 50, [(table, index, F)], [], F, work, 0, out=rows)
    collect_phase(k, o, rows, carry_phase(k, o, state, F, rows), F, dest)


def column_of(array):
    return lambda at: array[:, at, :].rearrange("p t a -> p (t a)")



def gin_layer(k, o, x, w):
    with layer(k):
        h, y = sb(k, None, "h", [P, NJ, D_IN]), sb(k, None, "y", [P, NJ, D_IN])
        a, b = sb(k, None, "a", [P, NJ, D_HID]), sb(k, None, "b", [P, NJ, D_HID])
        source = column_of(o.kept[0])
        norm_phase(k, x, h)
        aggregate(k, o, store_nodes_phase(k, h, D_IN), source, D_IN, y)
        add_phase(k, y, h)
        dense_phase(k, y, D_IN, w["W1a"][:], D_HID, a, w["b1a"][:], relu=True)
        dense_phase(k, a, D_HID, w["W2a"][:], D_HID, b, w["b2a"][:], relu=True)
        aggregate(k, o, store_nodes_phase(k, b, D_HID), source, D_HID, a)
        add_phase(k, a, b)
        dense_phase(k, a, D_HID, w["W1b"][:], D_HID, b, w["b1b"][:], relu=True)
        dense_phase(k, b, D_HID, w["W2b"][:], D_IN, y, w["b2b"][:])
        add_phase(k, x, y)


def attention_layer(k, o, x, w, r_feat):
    with layer(k):
        h, y = sb(k, None, "h", [P, NJ, D_IN]), sb(k, None, "y", [P, NJ, D_IN])
        e = sb(k, None, "e", [P, NE, HEADS])
        alpha = sb(k, None, "alpha", [P, NE, HEADS])
        en_rows = dram(k, "en_rows", [E, D_HID])
        norm_phase(k, x, h)
        with layer(k):
            a = sb(k, None, "a", [P, NJ, D_HID])
            dense_phase(k, h, D_IN, w["W2s"][:], D_HID, a, w["b2s"][:])
            sources = store_nodes_phase(k, a, D_HID)
            dense_phase(k, h, D_IN, w["W2d"][:], D_HID, a, w["b2d"][:])
            spread, head, _ = scatter_nodes_phase(k, o, a, D_HID)
            T = 50

            def scores(dve, c, at, got, read, tmp, res, exp):
                s, t = tmp
                for f in range(D_HID):
                    m = dve.tensor_tensor_scan(out=s[:, :, f], data0=o.same[:, at], data1=read[0][:, :, f],
                                               initial=head[:, f:f + 1], op0=ALU.mult, op1=ALU.add)
                c.after(m)
                c.after(dve.tensor_copy(head[:], s[:, T - 1, :]))
                c.after(dve.tensor_tensor(s[:], s[:], got[0][:], ALU.add))
                c.after(dve.scalar_tensor_tensor(t[:], s[:], 0.2, s[:], ALU.mult, ALU.max))
                c.after(dve.tensor_tensor(t[:], t[:], mid(w["attn"][:], T), ALU.mult))
                c.after(dve.tensor_reduce(e[:, at, :], t[:].rearrange("p t (h f) -> p t h f", h=HEADS), AX.X, ALU.add))
            edge_pass(k, o, T, [(sources, column_of(o.kept[0]), D_HID)], [(spread, D_HID)], 0, scores, 6,
                      keep=(0, en_rows), extra=[[D_HID], [D_HID]])

        expand_phase(k, o, segment_phase(k, o, e, HEADS, ALU.max), HEADS, alpha)
        nc = k.nc
        with phase(nc) as ph:
            own, exped = ph.sem("own"), ph.sem("exped")
            with nc.Block() as block:
                @block.vector
                def _(dve):
                    dve.tensor_tensor(e[:], e[:], alpha[:], ALU.subtract).then_inc(own, 1)

                @block.scalar
                def _(act):
                    act.wait_ge(own, 1)
                    nc.scalar.activation(e[:], e[:], ACT.Exp).then_inc(exped, 1)
        expand_phase(k, o, segment_phase(k, o, e, HEADS, ALU.add), HEADS, alpha)

        def divide(dve, c, ph):
            c.after(dve.tensor_scalar(alpha[:], alpha[:], 1e-9, None, ALU.max))
            c.after(dve.reciprocal(alpha[:], alpha[:]))
            dve.tensor_tensor(alpha[:], alpha[:], e[:], ALU.mult)
        dve_phase(k, divide)

        def messages(dve, c, at, got, read, tmp, res, exp):
            m, red, both = tmp
            v = m[:].rearrange("p t (h f) -> p (t h) f", h=HEADS)
            heads = red[:].rearrange("p t h -> p (t h)")
            to_exp, exped, n = exp
            c.after(dve.tensor_tensor(m[:], read[0][:], got[0][:], ALU.mult))
            c.after(dve.tensor_tensor(m[:].rearrange("p t (h f) -> p t h f", h=HEADS),
                                      m[:].rearrange("p t (h f) -> p t h f", h=HEADS),
                                      last(alpha[:, at, :], D_IN), ALU.mult))
            c.after(dve.tensor_reduce(heads, v, AX.X, ALU.max))
            dve.tensor_tensor(v, v, last(heads, D_IN), ALU.subtract).then_inc(to_exp, 1)
            dve.wait_ge(exped, n)
            c.after(dve.tensor_reduce(heads, v, AX.X, ALU.add))
            c.after(dve.reciprocal(red[:], red[:]))
            c.after(dve.tensor_tensor(v, v, last(heads, D_IN), ALU.mult))
            c.after(dve.tensor_tensor(both[:], m[:, :, 0:D_IN], m[:, :, D_IN:], ALU.add))
            return both
        rows = dram(k, "rows", [E + 1, D_IN])
        state = edge_pass(k, o, 50, [(r_feat, column_of(o.kept[1]), D_HID)], [(en_rows, D_HID)], D_IN, messages, 7,
                          out=rows, extra=[[D_HID], [HEADS], [D_IN]], exp_of=0)
        collect_phase(k, o, rows, carry_phase(k, o, state, D_IN, rows), D_IN, y)
        add_phase(k, h, y)
        dense_phase(k, h, D_IN, w["W1"][:], D_IN, y, w["b1"][:])
        add_phase(k, x, y)


def floor_clipped(dve, c, pos, clipped, q_i, top):
    c.after(dve.tensor_scalar(clipped, pos, 0.0, float(top), ALU.max, ALU.min))
    c.after(dve.tensor_copy(q_i[0], clipped))
    c.after(dve.tensor_copy(q_i[1], q_i[0]))
    c.after(dve.tensor_tensor(q_i[2], q_i[1], clipped, ALU.is_gt))
    c.after(dve.tensor_tensor(clipped, q_i[1], q_i[2], ALU.subtract))


def tent_layer(k, o, x, w):
    with layer(k):
        h, y = sb(k, None, "h", [P, NJ, D_IN]), sb(k, None, "y", [P, NJ, D_IN])
        norm_phase(k, x, h)
        table = dram(k, "patches", [N * 12, 2 * D_IN])
        table_phase(k, h, D_IN, w["tent_w"], D_IN, 4, 4, True, table)
        weights, index = sb(k, None, "weights", [P, NE, 4]), sb(k, None, "index", [P, NE], I32)
        uv = o.kept[1]

        def basis(dve, c, ph):
            pos, cell, q, g = (sb(k, ph, n, [P, NE, 2]) for n in ("pos", "cell", "q", "g"))
            q_i = sb(k, ph, "q_i", [P, NE, 2], I32)
            tents = [sb(k, ph, "tent", [P, NE, 2]) for _ in range(2)]
            flat = sb(k, ph, "flat", [P, NE])
            c.after(dve.tensor_scalar(pos[:], uv[:], 1.0, 1.5, ALU.add, ALU.mult))
            floor_clipped(dve, c, pos[:], cell[:], (q_i[:], q[:], g[:]), 2.5)
            for n in range(2):
                c.after(dve.tensor_scalar(q[:], cell[:], 2.0 / 3.0, -1.0 + n * 2.0 / 3.0, ALU.mult, ALU.add))
                c.after(dve.tensor_tensor(q[:], uv[:], q[:], ALU.subtract))
                c.after(dve.scalar_tensor_tensor(g[:], q[:], -1.0, q[:], ALU.mult, ALU.max))
                c.after(dve.tensor_scalar(g[:], g[:], -1.5, 1.0, ALU.mult, ALU.add))
                c.after(dve.tensor_scalar(tents[n][:], g[:], 0.0, None, ALU.max))
            for a in range(2):
                for b in range(2):
                    dve.tensor_tensor(weights[:, :, 2 * a + b], tents[a][:, :, 0], tents[b][:, :, 1], ALU.mult)
            c.after(dve.tensor_copy(flat[:], o.kept[0][:, :, 0]))
            c.after(dve.scalar_tensor_tensor(flat[:], flat[:], 3.0, cell[:, :, 1], ALU.mult, ALU.add))
            c.after(dve.scalar_tensor_tensor(flat[:], flat[:], 4.0, cell[:, :, 0], ALU.mult, ALU.add))
            dve.tensor_copy(index[:], flat[:])
        dve_phase(k, basis)
        rows = dram(k, "rows", [E + 1, D_IN])

        def work(dve, c, at, got, read, tmp, res, exp):
            v = got[0][:].rearrange("p t (c f) -> p t c f", c=4)
            c.after(dve.tensor_tensor(v, v, last(weights[:, at, :], D_IN), ALU.mult))
            c.after(dve.tensor_reduce(tmp[0][:], got[0][:].rearrange("p t (c f) -> p t f c", c=4), AX.X, ALU.add))
            return tmp[0]
        state = edge_pass(k, o, 50, [(table, lambda at: index[:, at], 4 * D_IN)], [], D_IN, work, 2, out=rows, extra=[[D_IN]])
        collect_phase(k, o, rows, carry_phase(k, o, state, D_IN, rows), D_IN, y)
        add_phase(k, x, y)


def spline_basis(k, pseudo, whole, frac, rest):
    def body(dve, c, ph):
        q, g = sb(k, ph, "q", [P, NE, 3]), sb(k, ph, "g", [P, NE, 3])
        q_i = sb(k, ph, "q_i", [P, NE, 3], I32)
        c.after(dve.tensor_scalar(frac[:], pseudo[:], 4.0, None, ALU.mult))
        floor_clipped(dve, c, frac[:], whole[:], (q_i[:], q[:], g[:]), 3)
        c.after(dve.tensor_tensor(frac[:], frac[:], whole[:], ALU.subtract))
        dve.tensor_scalar(rest[:], frac[:], -1.0, 1.0, ALU.mult, ALU.add)
    dve_phase(k, body)


SPAN = 7


def spline_conv(k, o, h, K, weight, C, paired, pseudo, dest, T):
    unit, gathers = (2 * C, 1) if paired else (C, 2)
    per_node = 4 * 25 if paired else K3
    table = dram(k, "corners", [N * per_node, unit])
    with layer(k):
        loaded_weight = sb(k, None, "conv_weight", [K, K3 * C])
        load_phase(k, loaded_weight[:].rearrange("p (a b) -> p a b", a=K3), weight)
        if paired:
            plain, loaded_weight = loaded_weight, sb(k, None, "turned_weight", [K, K3 * C])

            def permute(dve, c, ph):
                dve.tensor_copy(loaded_weight[:].rearrange("p (s g q) -> p g s q", s=5, g=5),
                                plain[:].rearrange("p (g s q) -> p g s q", s=5, g=5))
            dve_phase(k, permute)
        table_phase(k, h, K, loaded_weight, C, 25, 5, paired, table)
    with layer(k):
        index = [sb(k, None, "index", [P, NE], I32) for _ in range(gathers)]
        weight_rows = dram(k, "corner_weights", [E, 8])
        with layer(k):
            weights = sb(k, None, "weights", [P, NE, 8])
            whole, frac, rest = (sb(k, None, n, [P, NE, 3]) for n in ("whole", "frac", "rest"))
            spline_basis(k, pseudo, whole, frac, rest)

            def corners(dve, c, ph):
                pair, flat = sb(k, ph, "pair", [P, NE, 4]), sb(k, ph, "flat", [P, NE])
                side = (rest, frac)
                for b in range(2):
                    for d in range(2):
                        m = dve.tensor_tensor(pair[:, :, 2 * b + d], side[b][:, :, 1], side[d][:, :, 2], ALU.mult)
                c.after(m)
                for a in range(2):
                    dve.tensor_tensor(weights[:, :, 4 * a:4 * a + 4], pair[:], last(side[a][:, :, 0], 4), ALU.mult)
                c.after(dve.tensor_copy(flat[:], o.kept[0][:, :, 0]))
                for scale, d in ((4.0, 2), (5.0, 1), (5.0, 0)) if paired else ((5.0, 0), (5.0, 1), (5.0, 2)):
                    c.after(dve.scalar_tensor_tensor(flat[:], flat[:], scale, whole[:, :, d], ALU.mult, ALU.add))
                for a in range(gathers):
                    dve.tensor_scalar(index[a][:], flat[:], 25.0 * a, None, ALU.add)
            dve_phase(k, corners)
            load_phase(k, edges(weight_rows), weights[:])
        rows = dram(k, "rows", [E + 1, C])

        def work(dve, c, at, got, read, tmp, res, exp):
            for a in range(2):
                for b in range(2):
                    g = got[0 if paired else a]
                    first = b * 5 + a if paired else b * 5
                    v = window(g[:], first * unit, [(SPAN * unit, T), (C, 2), (1, C)])
                    of = last(read[0][:, :, 4 * a + 2 * b:4 * a + 2 * b + 2], C)
                    m = dve.tensor_tensor(v, v, of, ALU.mult)
            c.after(m)

            def corner(a, b, d):
                first = b * 5 + a if paired else b * 5
                return window(got[0 if paired else a][:], first * unit + d * C, [(SPAN * unit, T), (1, C)])
            for a in range(2):
                for b in range(2):
                    m = dve.tensor_tensor(corner(a, b, 0), corner(a, b, 0), corner(a, b, 1), ALU.add)
            c.after(m)
            for a in range(2):
                m = dve.tensor_tensor(corner(a, 0, 0), corner(a, 0, 0), corner(a, 1, 0), ALU.add)
            c.after(m)
            c.after(dve.tensor_tensor(corner(0, 0, 0), corner(0, 0, 0), corner(1, 0, 0), ALU.add))
            first = got[0][:]
            return first[:, :, 0:C]
        tables = [(table, lambda at, a=a: index[a][:, at], SPAN * unit) for a in range(gathers)]
        state = edge_pass(k, o, T, tables, [(weight_rows, 8)], C, work, 4, out=rows)
        collect_phase(k, o, rows, carry_phase(k, o, state, C, rows), C, dest)


def spline_layer(k, o, x, w):
    with layer(k):
        h, y = sb(k, None, "h", [P, NJ, D_IN]), sb(k, None, "y", [P, NJ, D_IN])
        v = sb(k, None, "v", [P, NJ, D_HID])
        pseudo = o.kept[2]
        norm_phase(k, x, h)
        with layer(k):
            whole, frac, rest = (sb(k, None, n, [P, NE, 3]) for n in ("whole", "frac", "rest"))
            spline_basis(k, pseudo, whole, frac, rest)
            sums = sb(k, None, "sums", [P, NJ, K3])
            rows = dram(k, "rows", [E + 1, K3])
            T = 25

            def work(dve, c, at, got, read, tmp, res, exp):
                u, u1, pair, full = tmp
                five = k.column[0:P, 0:5].unsqueeze(1).unsqueeze(1).broadcast_to([P, T, 3, 5])
                under = k.column_less[0:P, 0:5].unsqueeze(1).unsqueeze(1).broadcast_to([P, T, 3, 5])
                dve.tensor_tensor(u[:], five, last(whole[:, at, :], 5), ALU.is_equal)
                c.after(dve.tensor_tensor(u1[:], under, last(whole[:, at, :], 5), ALU.is_equal))
                dve.tensor_tensor(u[:], u[:], last(rest[:, at, :], 5), ALU.mult)
                c.after(dve.tensor_tensor(u1[:], u1[:], last(frac[:, at, :], 5), ALU.mult))
                c.after(dve.tensor_tensor(u[:], u[:], u1[:], ALU.add))
                c.after(dve.tensor_tensor(pair[:], last(u[:, :, 0, :], 5),
                                          u[:, :, 1, :].unsqueeze(2).broadcast_to([P, T, 5, 5]), ALU.mult))
                c.after(dve.tensor_tensor(full[:], last(pair[:].rearrange("p t a b -> p t (a b)"), 5),
                                          u[:, :, 2, :].unsqueeze(2).broadcast_to([P, T, 25, 5]), ALU.mult))
                return full[:].rearrange("p t a b -> p t (a b)")
            state = edge_pass(k, o, T, [], [], K3, work, 5, out=rows, extra=[[3, 5], [3, 5], [5, 5], [25, 5]])
            collect_phase(k, o, rows, carry_phase(k, o, state, K3, rows), K3, sums)
            dense_phase(k, sums, K3, w["stn1_w"][:], D_HID, v)
        elu_phase(k, v, D_HID, w["stn1_b"][0:P], o.degree)
        spline_conv(k, o, v, D_HID, k.stn2_w, D_HID, False, pseudo, v, 16)
        elu_phase(k, v, D_HID, w["stn2_b"][0:P], o.degree)
        with layer(k):
            u, t = sb(k, None, "u", [P, NJ, D_HID]), sb(k, None, "t", [P, NJ, 3])
            here, there = sb(k, None, "here", [P, NE, 3]), sb(k, None, "there", [P, NE, 3])
            dense_phase(k, v, D_HID, w["stn3_w"][:], D_HID, u, w["stn3_b"][:])
            elu_phase(k, u, D_HID)
            dense_phase(k, u, D_HID, w["stn4_w"][:], 3, t, w["stn4_b"][:])
            expand_phase(k, o, t, 3, here)
            table = store_nodes_phase(k, t, 3)

            def take(dve, c, at, got, read, tmp, res, exp):
                c.after(dve.tensor_copy(there[:, at, :], got[0][:]))
            edge_pass(k, o, 50, [(table, column_of(o.kept[0]), 3)], [], 0, take, 1)

            def shift(dve, c, ph):
                c.after(dve.tensor_tensor(pseudo[:], pseudo[:], there[:], ALU.add))
                c.after(dve.tensor_tensor(pseudo[:], pseudo[:], here[:], ALU.subtract))
                dve.tensor_scalar(pseudo[:], pseudo[:], 0.0, 1.0, ALU.max, ALU.min)
            dve_phase(k, shift)
        spline_conv(k, o, h, D_IN, k.conv_w, D_IN, True, pseudo, y, 20)

        def finish(dve, c, ph):
            mean_and_bias(dve, c, y, D_IN, w["conv_b"][0:P], o.degree, sb(k, ph, "d", [P, NJ]))
            dve.tensor_tensor(x[:], x[:], y[:], ALU.add)
        dve_phase(k, finish)


def program(nc, x, src, dst, edge_attr3_2x32, edge_attr_2, edge_attr_3, W1a, b1a, W2a, b2a, W1b, b1b, W2b, b2b,
            W1, b1, W2s, b2s, W2d, b2d, attn, tent_w, stn1_w, stn1_b, stn2_w, stn2_b, stn3_w, stn3_b,
            stn4_w, stn4_b, conv_w, conv_b, out, layers=4):
    k = Scope(None)
    k.nc = nc
    with ExitStack() as ctx:
        k.ctx = ctx
        as_row = lambda v: v.unsqueeze(0)
        weights = {
            "W1a": W1a, "b1a": as_row(b1a), "W2a": W2a, "b2a": as_row(b2a), "W1b": W1b, "b1b": as_row(b1b),
            "W2b": W2b, "b2b": as_row(b2b), "W1": W1, "b1": as_row(b1), "W2s": W2s, "b2s": as_row(b2s),
            "W2d": W2d, "b2d": as_row(b2d), "attn": across(attn.rearrange("a h f -> (a h f)"), P),
            "tent_w": tent_w.rearrange("a b i o -> i (a b) o"), "stn1_w": stn1_w.rearrange("k a o -> k (a o)"),
            "stn1_b": across(stn1_b, P), "stn2_b": across(stn2_b, P),
            "stn3_w": stn3_w, "stn3_b": as_row(stn3_b), "stn4_w": stn4_w, "stn4_b": as_row(stn4_b),
            "conv_b": across(conv_b, P),
        }
        constants_phase(k, weights)
        k.stn2_w, k.conv_w = stn2_w.rearrange("k i o -> i k o"), conv_w.rearrange("k i o -> i k o")
        xs = sb(k, None, "xs", [P, NJ, D_IN])
        with phase(nc) as ph:
            loaded = ph.sem("loaded")
            with nc.Block() as block:
                @block.sync
                def _(sp):
                    dma2(sp, xs[:], nodes(x), loaded)
                    sp.wait_ge(loaded, 32)
        one = lambda v: v.rearrange("(e a) -> e a", a=1)
        by_dst = sort_edges(k, dst, 4, [(one(dst), 1, I32, 0), (one(src), 1, I32, 1), (None, 1, I32, 2)])
        with layer(k):
            o = make_order(k, *by_dst, 4, [(1, 1, I32), (2, 1, I32)])
            gin_layer(k, o, xs, k.w)
            if layers > 1:
                attention_layer(k, o, xs, k.w, edge_attr3_2x32.rearrange("e h f -> e (h f)"))
        if layers > 2:
            by_src = sort_edges(k, src, 8, [(one(src), 1, I32, 0), (one(dst), 1, I32, 1), (edge_attr_2, 2, F32, 2),
                                            (edge_attr_3, 3, F32, 4)])
            with layer(k):
                o = make_order(k, *by_src, 8, [(1, 1, I32), (2, 2, F32), (4, 3, F32)])
                tent_layer(k, o, xs, k.w)
                if layers > 3:
                    spline_layer(k, o, xs, k.w)
        with phase(nc) as ph:
            stored = ph.sem("stored")
            with nc.Block() as block:
                @block.sync
                def _(sp):
                    dma2(sp, nodes(out), xs[:], stored)
                    sp.wait_ge(stored, 32)


_INS = ["x", "src", "dst", "edge_attr3_2x32", "edge_attr_2", "edge_attr_3",
        "L0_gnn_W1a", "L0_gnn_b1a", "L0_gnn_W2a", "L0_gnn_b2a", "L0_gnn_W1b", "L0_gnn_b1b", "L0_gnn_W2b", "L0_gnn_b2b",
        "L1_gnn_W1", "L1_gnn_b1", "L1_gnn_W2s", "L1_gnn_b2s", "L1_gnn_W2d", "L1_gnn_b2d", "L1_gnn_attn",
        "L2_gnn_weight", "L3_gnn_stn1_w", "L3_gnn_stn1_b", "L3_gnn_stn2_w", "L3_gnn_stn2_b", "L3_gnn_stn3_w",
        "L3_gnn_stn3_b", "L3_gnn_stn4_w", "L3_gnn_stn4_b", "L3_gnn_conv_w", "L3_gnn_conv_b"]


def kernel(**inputs):
    import numpy as _np
    import concourse.bacc as _bacc
    from concourse import mybir as _mybir
    from concourse.bass_utils import run_bass_kernel_spmd as _run

    nc = _bacc.Bacc("TRN2", target_bir_lowering=False, num_devices=1)
    arrays, args = {}, []
    for name in _INS:
        a = _np.ascontiguousarray(inputs[name])
        arrays[f"in_{name}_dram"] = a
        args.append(nc.dram_tensor(f"in_{name}_dram", a.shape, _mybir.dt.from_np(a.dtype), kind="ExternalInput").ap())
    args.append(nc.dram_tensor("out_dram", (N, D_IN), F32, kind="ExternalOutput").ap())
    program(nc, *args)
    r = _run(nc, [arrays], core_ids=[0])
    return r.results[0]["out_dram"]
```

```python
from contextlib import ExitStack, contextmanager

import concourse.bass as bass
import concourse.mybir as mybir
import numpy as np

F32 = mybir.dt.float32
BF16 = mybir.dt.bfloat16
I32 = mybir.dt.int32
ALU = mybir.AluOpType
ACT = mybir.ActivationFunctionType
AX = mybir.AxisListType

N, E, P = 6250, 100000, 125
NJ, NE = N // P, E // P
LO = 128
HI = -(-N // LO)
BIG = 1.0e30
FAR = 4 * E
D_IN, D_HID, HEADS = 32, 64, 2
K3 = 125


class Phase:

    def __init__(self, nc):
        self.nc, self.made = nc, []

    def sem(self, name):
        s = self.nc.alloc_semaphore(name=f"{name}_{self.nc.next_id()}")
        self.made.append(s)
        return s


@contextmanager
def phase(nc):
    ph = Phase(nc)
    with ExitStack() as ctx:
        ph.ctx = ctx
        yield ph
    nc.clear_and_free_semaphores(ph.made)
    nc.all_engine_barrier()


class Chain:

    def __init__(self, eng, sem):
        self.eng, self.sem, self.base, self.n = eng, sem, 0, 0

    def after(self, ins):
        ins.then_inc(self.sem, 1)
        self.n += 1
        self.eng.wait_ge(self.sem, self.base + self.n)

    def enter(self, i, steps):
        self.start, self.steps = self.base + self.n, steps
        self.base, self.n = self.start + i * steps, 0

    def leave(self, count):
        assert self.n == self.steps, (self.n, self.steps)
        self.base, self.n = self.start + count * self.steps, 0


def sb(k, ph, name, shape, dt=F32):
    ctx = ph.ctx if ph is not None else k.ctx
    return ctx.enter_context(k.nc.sbuf_tensor(f"{name}_{k.nc.next_id()}", shape, dt))


def pb(k, ph, name, shape, dt=F32):
    return ph.ctx.enter_context(k.nc.psum_tensor(f"{name}_{k.nc.next_id()}", shape, dt))


def dram(k, name, shape, dt=F32):
    return k.nc.dram_tensor(f"{name}_{k.nc.next_id()}", shape, dt).ap()


SPLIT = 112


def dma2(eng, out, in_, sem):
    eng.dma_start(out[0:SPLIT], in_[0:SPLIT]).then_inc(sem, 16)
    eng.dma_start(out[SPLIT:P], in_[SPLIT:P]).then_inc(sem, 16)


def edges(ap):
    return ap[0:E].rearrange("(p t) f -> p t f", t=NE)


def nodes(ap):
    return ap[0:N].rearrange("(p j) f -> p j f", j=NJ)


def mid(ap, n):
    return ap.unsqueeze(1).broadcast_to([ap.shape[0], n, ap.shape[1]])


def across(ap, n=128):
    return ap.unsqueeze(0).broadcast_to([n, ap.shape[0]])


def window(ap, offset, dims):
    return bass.AP(ap.tensor, ap.offset + offset, [list(ap.ap[0]), *[list(d) for d in dims]])


def last(ap, n):
    return ap.unsqueeze(len(ap.shape)).broadcast_to([*ap.shape, n])



def constants_phase(k, weights):
    nc = k.nc
    k.column = sb(k, None, "column", [128, 128])
    k.ident = sb(k, None, "ident", [128, 128])
    k.ident16 = sb(k, None, "ident16", [128, 128], BF16)
    k.before = sb(k, None, "before", [128, 128])
    k.ones = sb(k, None, "ones", [128, 128])
    k.column_less = sb(k, None, "column_less", [128, 8])
    k.w = {n: sb(k, None, n, [a.shape[0], int(np.prod(a.shape[1:]))]) for n, a in weights.items()}
    with phase(nc) as ph:
        col_i = sb(k, ph, "col_i", [128, 128], I32)
        diff_i = sb(k, ph, "diff_i", [128, 128], I32)
        diff = sb(k, ph, "diff", [128, 128])
        made, own, loaded = ph.sem("made"), ph.sem("own"), ph.sem("loaded")
        with nc.Block() as block:
            @block.gpsimd
            def _(pool):
                nc.gpsimd.iota(col_i[:], pattern=[[1, 128]], base=0, channel_multiplier=0)
                nc.gpsimd.iota(diff_i[:], pattern=[[1, 128]], base=0, channel_multiplier=-1).then_inc(made, 1)

            @block.sync
            def _(sp):
                for n, a in weights.items():
                    to = k.w[n][:]
                    if len(a.shape) == 3:
                        to = to.rearrange("p (a b) -> p a b", a=a.shape[1])
                    sp.dma_start(to, a).then_inc(loaded, 16)
                sp.wait_ge(loaded, 16 * len(weights))

            @block.vector
            def _(dve):
                c = Chain(dve, own)
                dve.wait_ge(made, 1)
                dve.memset(k.ones[:], 1.0)
                dve.tensor_copy(k.column[:], col_i[:])
                c.after(dve.tensor_copy(diff[:], diff_i[:]))
                dve.tensor_scalar(k.column_less[:], k.column[:, 0:8], -1.0, None, ALU.add)
                dve.tensor_scalar(k.ident[:], diff[:], 0.0, None, ALU.is_equal)
                dve.tensor_scalar(k.ident16[:], diff[:], 0.0, None, ALU.is_equal)
                c.after(dve.tensor_scalar(k.before[:], diff[:], 0.0, None, ALU.is_gt))



GT = 8


def split_keys(dve, c, key_i, hi_i, lo_i, hi, lo):
    c.after(dve.tensor_scalar(hi_i[:], key_i[:], 7, None, ALU.logical_shift_right))
    c.after(dve.tensor_scalar(lo_i[:], key_i[:], LO - 1, None, ALU.bitwise_and))
    dve.tensor_copy(hi[:], hi_i[:])
    c.after(dve.tensor_copy(lo[:], lo_i[:]))


def sort_edges(k, key_dram, width, fill):
    nc = k.nc
    rows = dram(k, "sorted_rows", [E, width])
    first_of, count_of = dram(k, "first_of", [HI, LO]), dram(k, "count_of", [HI, LO])
    with ExitStack() as ctx:
        scope = Scope(ctx)
        hi, lo = sb(k, scope, "hi", [P, NE + GT]), sb(k, scope, "lo", [P, NE + GT])
        row = sb(k, scope, "row", [P, NE, width])
        base = sb(k, scope, "base", [LO, HI])
        count_s = sb(k, scope, "count_s", [LO, HI])
        is_lo = sb(k, scope, "is_lo", [P, 2, GT, LO], BF16)
        is_hi = sb(k, scope, "is_hi", [P, 2, GT, HI], BF16)
        load_keys_phase(k, key_dram, fill, hi, lo, row)
        count_phase(k, hi, lo, is_lo, is_hi, count_s)
        prefix_phase(k, count_s, base, first_of, count_of)
        place_phase(k, hi, lo, is_lo, is_hi, base, row, rows, width)
    return rows, first_of, count_of


class Scope:

    def __init__(self, ctx):
        self.ctx = ctx


def load_keys_phase(k, key_dram, fill, hi, lo, row):
    nc = k.nc
    with phase(nc) as ph:
        key_i, half = sb(k, ph, "key_i", [P, NE], I32), sb(k, ph, "half", [P, 2, NE], I32)
        parts = [sb(k, ph, "part", [P, NE, f], dt) for _, f, dt, _ in fill]
        loaded, numbered, own = ph.sem("loaded"), ph.sem("numbered"), ph.sem("own")
        loads = 1 + sum(src is not None for src, *_ in fill)
        with nc.Block() as block:
            @block.sync
            def _(sp):
                sp.dma_start(key_i[:], key_dram.rearrange("(p t) -> p t", t=NE)).then_inc(loaded, 16)
                for part, (src, f, _, _) in zip(parts, fill):
                    if src is not None:
                        sp.dma_start(part[:], src.rearrange("(p t) f -> p t f", t=NE)).then_inc(loaded, 16)

            @block.gpsimd
            def _(pool):
                for part, (src, *_) in zip(parts, fill):
                    if src is None:
                        nc.gpsimd.iota(part[:, :, 0], pattern=[[1, NE]], base=0,
                                       channel_multiplier=NE).then_inc(numbered, 1)

            @block.vector
            def _(dve):
                c = Chain(dve, own)
                dve.memset(hi[:, NE:], 0.0)
                dve.memset(lo[:, NE:], 0.0)
                c.after(dve.memset(row[:], 0.0))
                dve.wait_ge(loaded, 16 * loads)
                if loads <= len(fill):
                    dve.wait_ge(numbered, 1)
                dve.tensor_scalar(half[:, 0], key_i[:], 7, None, ALU.logical_shift_right)
                c.after(dve.tensor_scalar(half[:, 1], key_i[:], LO - 1, None, ALU.bitwise_and))
                dve.tensor_copy(hi[:, 0:NE], half[:, 0])
                dve.tensor_copy(lo[:, 0:NE], half[:, 1])
                for part, (_, f, _, at) in zip(parts, fill):
                    dve.tensor_copy(row[:, :, at:at + f], part[:])


def one_hots(k, dve, hi, lo, is_hi, is_lo, i, n):
    g, b = (i * 2 + n) * GT, n % 2
    dve.tensor_tensor(is_lo[:, b], mid(k.column[0:P, 0:LO], GT), last(lo[:, bass.ds(g, GT)], LO), ALU.is_equal)
    return dve.tensor_tensor(is_hi[:, b], mid(k.column[0:P, 0:HI], GT), last(hi[:, bass.ds(g, GT)], HI), ALU.is_equal)


def count_phase(k, hi, lo, is_lo, is_hi, count_s):
    nc = k.nc
    with phase(nc) as ph:
        zero16 = sb(k, ph, "zero16", [P, LO], BF16)
        count_p = pb(k, ph, "count_p", [LO, HI])
        zeroed, hot, counted = ph.sem("zeroed"), ph.sem("hot"), ph.sem("counted")
        with nc.Block() as block:
            @block.vector
            def _(dve):
                dve.memset(zero16[:], 0.0).then_inc(zeroed, 1)
                with dve.Fori(0, NE // GT // 2) as i:
                    for b in range(2):
                        dve.wait_ge(counted, i * 2 + b)
                        one_hots(k, dve, hi, lo, is_hi, is_lo, i, b).then_inc(hot, 1)
                dve.wait_ge(counted, NE // GT + 2)
                dve.tensor_copy(count_s[:], count_p[:])

            @block.tensor
            def _(pe):
                pe.wait_ge(zeroed, 1)
                nc.tensor.matmul(count_p[:], zero16[:], zero16[:, 0:HI], start=True, stop=False).then_inc(counted, 1)
                with pe.Fori(0, NE // GT // 2) as i:
                    for b in range(2):
                        pe.wait_ge(hot, i * 2 + b + 1)
                        for t in range(GT):
                            m = nc.tensor.matmul(count_p[:], is_lo[:, b, t, :], is_hi[:, b, t, :],
                                                 start=False, stop=False)
                        m.then_inc(counted, 1)
                nc.tensor.matmul(count_p[:], zero16[:], zero16[:, 0:HI], start=False, stop=True).then_inc(counted, 1)


def prefix_phase(k, count_s, base, first_of, count_of):
    nc = k.nc
    with phase(nc) as ph:
        below_p, total_p = pb(k, ph, "below_p", [LO, HI]), pb(k, ph, "total_p", [LO, HI])
        turned_p = pb(k, ph, "turned_p", [HI, 2, LO])
        total_s, upto = sb(k, ph, "total_s", [LO, HI]), sb(k, ph, "upto", [LO, HI])
        turned = sb(k, ph, "turned", [HI, 2, LO])
        summed, own, turns, copied, stored = (ph.sem(n) for n in ("summed", "own", "turns", "copied", "stored"))
        with nc.Block() as block:
            @block.tensor
            def _(pe):
                nc.tensor.matmul(below_p[:], k.before[:], count_s[:], start=True, stop=True)
                nc.tensor.matmul(total_p[:], k.ones[:], count_s[:], start=True, stop=True).then_inc(summed, 1)
                pe.wait_ge(own, 4)
                nc.tensor.transpose(turned_p[:, 0, :], base[:], k.ident[:])
                nc.tensor.transpose(turned_p[:, 1, :], count_s[:], k.ident[:]).then_inc(turns, 1)

            @block.vector
            def _(dve):
                c = Chain(dve, own)
                dve.wait_ge(summed, 1)
                c.after(dve.tensor_copy(total_s[:], total_p[:]))
                c.after(dve.tensor_tensor_scan(out=upto[:], data0=k.ones[:, 0:HI], data1=total_s[:], initial=0.0,
                                               op0=ALU.mult, op1=ALU.add))
                c.after(dve.tensor_tensor(upto[:], upto[:], total_s[:], ALU.subtract))
                c.after(dve.tensor_tensor(base[:], upto[:], below_p[:], ALU.add))
                dve.wait_ge(turns, 1)
                dve.tensor_copy(turned[:], turned_p[:]).then_inc(copied, 1)

            @block.sync
            def _(sp):
                sp.wait_ge(copied, 1)
                sp.dma_start(first_of, turned[:, 0, :]).then_inc(stored, 16)
                sp.dma_start(count_of, turned[:, 1, :]).then_inc(stored, 16)
                sp.wait_ge(stored, 32)


def place_phase(k, hi, lo, is_lo, is_hi, base, row, rows, width):
    nc = k.nc
    half = GT // 2
    pairs = NE // GT // 2
    with phase(nc) as ph:
        turned_p = pb(k, ph, "turned_p", [LO, GT, 128], BF16)
        match_p = [pb(k, ph, f"match_p{b}", [P, half, P]) for b in range(2)]
        rank_p = [pb(k, ph, f"rank_p{b}", [P, GT, HI]) for b in range(2)]
        next_p = pb(k, ph, "next_p", [LO, GT + 1, HI])
        lo_t = sb(k, ph, "lo_t", [LO, GT, P])
        lo_t16 = sb(k, ph, "lo_t16", [LO, GT, P], BF16)
        earlier = sb(k, ph, "earlier", [P, 2, half, P], BF16)
        next_s = [sb(k, ph, "next_s", [LO, GT + 1, HI]) for _ in range(2)]
        picked, pos = sb(k, ph, "picked", [P, GT, HI]), sb(k, ph, "pos", [P, GT])
        pos_i = [sb(k, ph, "pos_i", [P, GT], I32) for _ in range(2)]
        row_now = [sb(k, ph, "row_now", [P, GT, width]) for _ in range(2)]
        names = ("hot", "turned", "copied", "matched", "masked", "begun", "moved", "snapped", "ranked", "own", "placed", "seen")
        hot, turned, copied, matched, masked, begun, moved, snapped, ranked, own, placed, seen = (ph.sem(n) for n in names)
        scattered = [ph.sem("scattered0"), ph.sem("scattered1")]
        with nc.Block() as block:
            @block.vector
            def _(dve):
                c = Chain(dve, own)
                dve.tensor_copy(next_s[1][:, GT, :], base[:]).then_inc(begun, 1)
                one_hots(k, dve, hi, lo, is_hi, is_lo, 0, 0).then_inc(hot, 1)
                with dve.Fori(0, pairs) as i:
                    c.enter(i, 4)
                    for b in range(2):
                        g = i * 2 + b
                        dve.wait_ge(ranked, g)
                        one_hots(k, dve, hi, lo, is_hi, is_lo, i, b + 1).then_inc(hot, 1)
                        for h in range(2):
                            dve.wait_ge(matched, g * 2 + h + 1)
                            dve.tensor_tensor(earlier[:, h], match_p[h][:], mid(k.before[0:P, 0:P], half),
                                              ALU.mult).then_inc(masked, 1)
                        dve.wait_ge(ranked, g + 1)
                        c.after(dve.tensor_tensor(picked[:], rank_p[b][:], is_hi[:, b], ALU.mult))
                        c.after(dve.tensor_reduce(pos[:], picked[:], AX.X, ALU.add))
                        dve.wait_ge(scattered[b], i * (16 * GT))
                        dve.tensor_copy(pos_i[b][:], pos[:])
                        dve.tensor_copy(row_now[b][:], row[:, bass.ds(g * GT, GT), :]).then_inc(placed, 1)
                    c.leave(pairs)

            @block.scalar
            def _(act):
                with act.Fori(0, pairs) as i:
                    for b in range(2):
                        g = i * 2 + b
                        act.wait_ge(turned, g + 1)
                        act.wait_ge(ranked, g)
                        nc.scalar.copy(lo_t16[:], turned_p[:, :, 0:P]).then_inc(copied, 1)
                        nc.scalar.copy(lo_t[:], turned_p[:, :, 0:P]).then_inc(copied, 1)
                        act.wait_ge(moved, g + 1)
                        nc.scalar.copy(next_s[b][:], next_p[:]).then_inc(snapped, 1)

            @block.tensor
            def _(pe):
                pe.wait_ge(begun, 1)
                with pe.Fori(0, pairs) as i:
                    for b in range(2):
                        g = i * 2 + b
                        pe.wait_ge(hot, g + 1)
                        pe.wait_ge(copied, g * 2)
                        for t in range(GT):
                            m = nc.tensor.transpose(turned_p[:, t, 0:P], is_lo[:, b, t, :], k.ident16[0:P, 0:P])
                        m.then_inc(turned, 1)
                        pe.wait_ge(snapped, g)
                        for t in range(GT + 1):
                            m = nc.tensor.matmul(next_p[:, t, :], k.ident[:], next_s[1 - b][:, GT, :], start=True, stop=t == 0)
                            for u in range(t):
                                m = nc.tensor.matmul(next_p[:, t, :], is_lo[:, b, u, :], is_hi[:, b, u, :],
                                                     start=False, stop=u == t - 1)
                        m.then_inc(moved, 1)
                        pe.wait_ge(copied, g * 2 + 1)
                        pe.wait_ge(masked, g * 2)
                        for h in range(2):
                            for t in range(half):
                                one = lo_t16[:, h * half + t, :]
                                m = nc.tensor.matmul(match_p[h][:, t, :], one, one, start=True, stop=True)
                            m.then_inc(matched, 1)
                        pe.wait_ge(copied, g * 2 + 2)
                        pe.wait_ge(snapped, g + 1)
                        for t in range(GT):
                            if t % half == 0:
                                pe.wait_ge(masked, g * 2 + 1 + t // half)
                            nc.tensor.matmul(rank_p[b][:, t, :], lo_t[:, t, :], next_s[b][:, t, :], start=True, stop=False)
                            m = nc.tensor.matmul(rank_p[b][:, t, :], earlier[:, t // half, t % half, :],
                                                 is_hi[:, b, t, :], start=False, stop=True)
                        m.then_inc(ranked, 1)

            @block.gpsimd
            def _(pool):
                with pool.Fori(0, pairs) as i:
                    for b in range(2):
                        pool.wait_ge(placed, i * 2 + b + 1)
                        pool.sem_inc(seen, 1)
                        for t in range(GT):
                            pool.indirect_dma_start(
                                out=rows, out_offset=bass.IndirectOffsetOnAxis(ap=pos_i[b][:, t:t + 1], axis=0),
                                in_=row_now[b][:, t, :], in_offset=None).then_inc(scattered[b], 16)
                for b in range(2):
                    pool.wait_ge(scattered[b], pairs * 16 * GT)



class Order:
    pass


def make_order(k, rows, first_of, count_of, width, take):
    nc, o = k.nc, Order()
    o.same = sb(k, None, "same", [P, NE])
    o.carry = sb(k, None, "carry", [64 * 2, P])
    o.end = sb(k, None, "end", [P, NJ], I32)
    o.fix = sb(k, None, "fix", [P, 1], I32)
    o.first = sb(k, None, "first", [P, NJ], I32)
    o.degree = sb(k, None, "degree", [P, NJ])
    o.head = sb(k, None, "head", [P, 1], I32)
    o.kept = [sb(k, None, "kept", [P, NE, f], dt) for _, f, dt in take]
    carry_d = dram(k, "carry", [P, 1])
    with phase(nc) as ph:
        row = sb(k, ph, "row", [P, NE, width])
        key = sb(k, ph, "key", [P, NE + 1])
        pass_on = sb(k, ph, "pass_on", [P, 1])
        first, t1, t2, some = (sb(k, ph, n, [P, NJ]) for n in ("first", "t1", "t2", "some"))
        run, fix = sb(k, ph, "run", [P, NE]), sb(k, ph, "fix", [P, 1])
        begin, begin_i = sb(k, ph, "begin", [P, 1]), sb(k, ph, "begin_i", [P, 1], I32)
        numbered = ph.sem("numbered")
        loaded, own, ready, stored, spread = (ph.sem(n) for n in ("loaded", "own", "ready", "stored", "spread"))
        with nc.Block() as block:
            @block.sync
            def _(sp):
                dma2(sp, row[:], edges(rows), loaded)
                sp.dma_start(first[:], first_of.rearrange("h l -> (h l)")[0:N].rearrange("(p j) -> p j", j=NJ)).then_inc(loaded, 16)
                sp.dma_start(o.degree[:], count_of.rearrange("h l -> (h l)")[0:N].rearrange("(p j) -> p j", j=NJ)).then_inc(loaded, 16)
                sp.wait_ge(ready, 1)
                sp.dma_start(key[1:P, 0:1], edges(rows)[0:P - 1, NE - 1, 0:1],
                             allow_slow_non_contiguous=True).then_inc(loaded, 16)
                sp.wait_ge(ready, 2)
                sp.dma_start(carry_d, pass_on[:]).then_inc(stored, 16)
                sp.wait_ge(stored, 16)
                sp.dma_start(o.carry[:], across(carry_d.rearrange("p f -> (p f)"))).then_inc(spread, 16)
                sp.wait_ge(spread, 16)

            @block.gpsimd
            def _(pool):
                nc.gpsimd.iota(begin_i[:], pattern=[[1, 1]], base=0, channel_multiplier=1).then_inc(numbered, 1)

            @block.vector
            def _(dve):
                c = Chain(dve, own)
                dve.memset(key[:, 0:1], -1.0).then_inc(ready, 1)
                dve.wait_ge(loaded, 80)
                c.after(dve.tensor_copy(key[:, 1:], row[:, :, 0]))
                dve.wait_ge(numbered, 1)
                c.after(dve.tensor_copy(begin[:], begin_i[:]))
                dve.tensor_copy(o.head[:], key[:, 1:2])
                c.after(dve.tensor_tensor(o.same[:], key[:, 1:], key[:, 0:NE], ALU.is_equal))
                c.after(dve.tensor_tensor(pass_on[:], key[:, 1:2], key[:, NE:NE + 1], ALU.is_equal))
                dve.tensor_tensor(pass_on[:], pass_on[:], o.same[:, 0:1], ALU.mult).then_inc(ready, 1)
                for kept, (at, f, _) in zip(o.kept, take):
                    dve.tensor_copy(kept[:], row[:, :, at:at + f])
                c.after(dve.tensor_scalar(some[:], o.degree[:], 0.0, None, ALU.is_gt))
                c.after(dve.tensor_scalar(t1[:], some[:], -float(FAR), float(FAR), ALU.mult, ALU.add))
                c.after(dve.tensor_tensor(o.first[:], t1[:], first[:], ALU.add))
                c.after(dve.tensor_tensor(t1[:], first[:], o.degree[:], ALU.add))
                c.after(dve.tensor_scalar(t1[:], t1[:], -float(E + 1), None, ALU.add))
                c.after(dve.tensor_tensor(t1[:], t1[:], some[:], ALU.mult))
                c.after(dve.tensor_scalar(t1[:], t1[:], float(E), None, ALU.add))
                c.after(dve.tensor_copy(o.end[:], t1[:]))
                c.after(dve.tensor_tensor_scan(out=run[:], data0=o.same[:], data1=o.same[:], initial=1.0,
                                               op0=ALU.mult, op1=ALU.min))
                c.after(dve.tensor_reduce(run[:, 0:1], run[:], AX.X, ALU.add))
                c.after(dve.tensor_scalar(fix[:], run[:, 0:1], 0.5, float(FAR), ALU.is_lt, ALU.mult))
                c.after(dve.tensor_tensor(fix[:], fix[:], run[:, 0:1], ALU.add))
                c.after(dve.scalar_tensor_tensor(fix[:], begin[:], float(NE), fix[:], ALU.mult, ALU.add))
                c.after(dve.tensor_scalar(fix[:], fix[:], -1.0, None, ALU.add))
                c.after(dve.tensor_copy(o.fix[:], fix[:]))
    return o



def edge_pass(k, o, T, tables, streams, F, work, steps, out=None, keep=None, extra=(), exp_of=None, beside=None):
    nc = k.nc
    pairs = NE // T // 2
    state = sb(k, None, "state", [P, max(F, 1)]) if F else None
    with phase(nc) as ph:
        got = [[sb(k, ph, "got", [P, T, w]) for _ in range(2)] for _, _, w in tables]
        read = [[sb(k, ph, "read", [P, T, w]) for _ in range(2)] for _, w in streams]
        res = [sb(k, ph, "res", [P, T, F]) for _ in range(2)] if F else None
        idx = [[sb(k, ph, "idx", [P, T], I32) for _ in range(2)] for _ in tables]
        tmp = [sb(k, ph, "tmp", [P, T, *shape]) for shape in extra]
        indexed, seen, own, done, exped = (ph.sem(n) for n in ("indexed", "seen", "own", "done", "exped"))
        gathered, loaded, stored, used = ([ph.sem(f"{n}{b}") for b in range(2)] for n in ("gathered", "loaded", "stored", "used"))
        to_exp, ready = ph.sem("to_exp"), ph.sem("ready")
        other = Table(k, ph, *beside) if beside else None
        stores = 32 * (bool(out is not None) + bool(keep))
        with nc.Block() as block:
            if tables:
                @block.gpsimd
                def _(pool):
                    with pool.Fori(0, pairs) as i:
                        for b in range(2):
                            g = i * 2 + b
                            pool.wait_ge(used[b], i)
                            if keep:
                                pool.wait_ge(stored[b], i * stores)
                            for n, (_, index, _) in enumerate(tables):
                                pool.tensor_copy(idx[n][b][:], index(bass.ds(g * T, T))).then_inc(indexed, 1)
                            pool.wait_ge(indexed, (g + 1) * len(tables))
                            pool.sem_inc(seen, 1)
                            for n, (table, _, _) in enumerate(tables):
                                for t in range(T):
                                    pool.indirect_dma_start(
                                        out=got[n][b][:, t, :], out_offset=None, in_=table,
                                        in_offset=bass.IndirectOffsetOnAxis(ap=idx[n][b][:, t:t + 1], axis=0)
                                    ).then_inc(gathered[b], 16)

            @block.sync
            def _(sp):
                def load(g, b):
                    for n, (rows, _) in enumerate(streams):
                        dma2(sp, read[n][b][:], edges(rows)[:, bass.ds(g * T, T), :], loaded[b])

                if streams:
                    for b in range(2):
                        load(b, b)

                def chunks(i, more):
                    for b in range(2):
                        g = i * 2 + b
                        if keep:
                            sp.wait_ge(gathered[b], (i + 1) * (16 * T * len(tables)))
                            sp.sem_inc(ready, 1)
                            dma2(sp, edges(keep[1])[:, bass.ds(g * T, T), :], got[keep[0]][b][:], stored[b])
                        sp.wait_ge(done, g + 1)
                        sp.sem_inc(ready, 1)
                        if out is not None:
                            dma2(sp, edges(out)[:, bass.ds(g * T, T), :], res[b][:], stored[b])
                        if streams and more:
                            load(g + 2, b)
                with sp.Fori(0, pairs - 1) as i:
                    chunks(i, True)
                chunks(pairs - 1, False)
                if stores:
                    for b in range(2):
                        sp.wait_ge(stored[b], pairs * stores)
            @block.vector
            def _(dve):
                c = Chain(dve, own)
                if F:
                    c.after(dve.memset(state[:], 0.0))
                with dve.Fori(0, pairs) as i:
                    c.enter(i, 2 * (steps + (2 if F else 0)))
                    for b in range(2):
                        if tables:
                            dve.wait_ge(gathered[b], (i + 1) * (16 * T * len(tables)))
                        if streams:
                            dve.wait_ge(loaded[b], (i + 1) * (32 * len(streams)))
                        if out is not None:
                            dve.wait_ge(stored[b], i * stores)
                        at = bass.ds((i * 2 + b) * T, T)
                        src = work(dve, c, at, [x[b] for x in got], [x[b] for x in read], tmp,
                                   res[b] if F else None, (to_exp, exped, i * 2 + b + 1))
                        if F:
                            for f in range(F):
                                m = dve.tensor_tensor_scan(out=res[b][:, :, f], data0=o.same[:, at], data1=src[:, :, f],
                                                           initial=state[:, f:f + 1], op0=ALU.mult, op1=ALU.add)
                            c.after(m)
                            dve.tensor_copy(state[:], res[b][:, T - 1, :]).then_inc(own, 1)
                            c.n += 1
                            dve.wait_ge(own, c.base + c.n)
                        dve.sem_inc(used[b], 1)
                        dve.sem_inc(done, 1)
                    c.leave(pairs)

            @block.scalar
            def _(act):
                if other:
                    other.scalar(act)
                if exp_of is not None:
                    with act.Fori(0, pairs) as i:
                        for b in range(2):
                            act.wait_ge(to_exp, i * 2 + b + 1)
                            nc.scalar.activation(tmp[exp_of][:], tmp[exp_of][:], ACT.Exp).then_inc(exped, 1)

            @block.tensor
            def _(pe):
                if other:
                    other.tensor(pe)
    return state


def carry_phase(k, o, state, F, rows, op=ALU.add, zero=0.0):
    nc = k.nc
    with phase(nc) as ph:
        state_p = pb(k, ph, "state_p", [F, P])
        back_p = pb(k, ph, "back_p", [P, F])
        state_t, total_t = sb(k, ph, "state_t", [F, P]), sb(k, ph, "total_t", [F, P + 1])
        flags = sb(k, ph, "flags", [F, P])
        now, nothing = sb(k, ph, "now", [P, F]), sb(k, ph, "nothing", [1, F])
        own, turned, back, cleared, ready, stored, fixed = (
            ph.sem(n) for n in ("own", "turned", "back", "cleared", "ready", "stored", "fixed"))
        with nc.Block() as block:
            @block.tensor
            def _(pe):
                nc.tensor.transpose(state_p[:], state[:], k.ident[0:P, 0:P]).then_inc(turned, 1)
                pe.wait_ge(own, 4)
                nc.tensor.transpose(back_p[:], total_t[:, 0:P], k.ident[0:F, 0:F]).then_inc(back, 1)

            @block.vector
            def _(dve):
                c = Chain(dve, own)
                dve.memset(now[:], 0.0).then_inc(cleared, 1)
                dve.memset(total_t[:, 0:1], zero)
                c.after(dve.memset(nothing[:], zero))
                if op == ALU.max:
                    c.after(dve.tensor_scalar(flags[:], o.carry[0:F, :], BIG, -BIG, ALU.mult, ALU.add))
                else:
                    c.after(dve.tensor_copy(flags[:], o.carry[0:F, :]))
                dve.wait_ge(turned, 1)
                c.after(dve.tensor_copy(state_t[:], state_p[:]))
                c.after(dve.tensor_tensor_scan(out=total_t[:, 1:], data0=flags[:], data1=state_t[:], initial=zero,
                                               op0=ALU.add if op == ALU.max else ALU.mult, op1=op))
                dve.wait_ge(back, 1)
                dve.wait_ge(fixed, 16)
                dve.tensor_tensor(now[:], now[:], back_p[:], op).then_inc(ready, 1)

            @block.gpsimd
            def _(pool):
                at = bass.IndirectOffsetOnAxis(ap=o.fix[:], axis=0)
                pool.wait_ge(cleared, 1)
                pool.indirect_dma_start(out=now[:], out_offset=None, in_=rows, in_offset=at,
                                        bounds_check=E - 1, oob_is_err=False).then_inc(fixed, 16)
                pool.wait_ge(ready, 1)
                pool.indirect_dma_start(out=rows, out_offset=at, in_=now[:], in_offset=None,
                                        bounds_check=E - 1, oob_is_err=False).then_inc(fixed, 16)
                pool.wait_ge(fixed, 32)

            @block.sync
            def _(sp):
                sp.wait_ge(own, 1)
                sp.dma_start(rows[E:E + 1, :], nothing[:]).then_inc(stored, 16)
                sp.wait_ge(stored, 16)


def collect_phase(k, o, rows, F, dest):
    nc = k.nc
    with phase(nc) as ph:
        gathered = ph.sem("gathered")
        with nc.Block() as block:
            @block.gpsimd
            def _(pool):
                for j in range(NJ):
                    pool.indirect_dma_start(
                        out=dest[:, j, :], out_offset=None, in_=rows,
                        in_offset=bass.IndirectOffsetOnAxis(ap=o.end[:, j:j + 1], axis=0)).then_inc(gathered, 16)
                pool.wait_ge(gathered, 16 * NJ)


def scatter_nodes_phase(k, o, src, F):
    nc = k.nc
    spread, table = dram(k, "spread", [E, F]), dram(k, "node_rows", [N, F])
    head = sb(k, None, "head_row", [P, F])
    cols = 3200 // F if F in (32, 64) else 800
    with phase(nc) as ph:
        zeros = sb(k, ph, "zeros", [P, cols, F])
        zeroed = ph.sem("zeroed")
        cleared, stored, scattered = ph.sem("cleared"), ph.sem("stored"), ph.sem("scattered")
        pieces = NE // cols
        with nc.Block() as block:
            @block.vector
            def _(dve):
                dve.memset(zeros[:], 0.0).then_inc(zeroed, 1)

            @block.sync
            def _(sp):
                sp.wait_ge(zeroed, 1)
                for n in range(pieces):
                    dma2(sp, edges(spread)[:, n * cols:(n + 1) * cols, :], zeros[:], cleared)

            @block.scalar
            def _(act):
                act.dma_start(nodes(table), src[:]).then_inc(stored, 16)
                act.wait_ge(stored, 16)

            @block.gpsimd
            def _(pool):
                pool.wait_ge(cleared, 32 * pieces)
                for j in range(NJ):
                    pool.indirect_dma_start(
                        out=spread, out_offset=bass.IndirectOffsetOnAxis(ap=o.first[:, j:j + 1], axis=0),
                        in_=src[:, j, :], in_offset=None, bounds_check=E - 1, oob_is_err=False).then_inc(scattered, 16)
                pool.wait_ge(stored, 16)
                pool.indirect_dma_start(out=head[:], out_offset=None, in_=table,
                                        in_offset=bass.IndirectOffsetOnAxis(ap=o.head[:], axis=0)).then_inc(scattered, 16)
                pool.wait_ge(scattered, 16 * (NJ + 1))
    return spread, head, table


def store_nodes_phase(k, src, F):
    nc = k.nc
    table = dram(k, "node_rows", [N, F])
    with phase(nc) as ph:
        stored = ph.sem("stored")
        with nc.Block() as block:
            @block.sync
            def _(sp):
                sp.dma_start(nodes(table), src[:]).then_inc(stored, 16)
                sp.wait_ge(stored, 16)
    return table



JG = 5


def dense_phase(k, src, K, weight, C, dest, bias=None, relu=False):
    nc = k.nc
    pairs = NJ // JG // 2
    with phase(nc) as ph:
        now = [sb(k, ph, "now", [P, JG, K]) for _ in range(2)]
        turned = [sb(k, ph, "turned", [K, JG, P]) for _ in range(2)]
        turned_p = [pb(k, ph, f"turned_p{b}", [K, JG, 128]) for b in range(2)]
        made_p = [pb(k, ph, f"made_p{b}", [P, JG, C]) for b in range(2)]
        taken, seen, flipped, copied, made, out = (ph.sem(n) for n in ("taken", "seen", "flipped", "copied", "made", "out"))
        with nc.Block() as block:
            @block.vector
            def _(dve):
                with dve.Fori(0, pairs) as i:
                    for b in range(2):
                        g = i * 2 + b
                        dve.wait_ge(copied, i * 2)
                        dve.tensor_copy(now[b][:], src[:, bass.ds(g * JG, JG), :]).then_inc(taken, 1)
                        dve.wait_ge(made, g + 1)
                        o = dest[:, bass.ds(g * JG, JG), :]
                        if relu:
                            dve.tensor_scalar(o, made_p[b][:], 0.0, None, ALU.max).then_inc(out, 1)
                        else:
                            dve.tensor_copy(o, made_p[b][:]).then_inc(out, 1)

            @block.tensor
            def _(pe):
                with pe.Fori(0, pairs) as i:
                    for b in range(2):
                        g = i * 2 + b
                        pe.wait_ge(taken, g + 1)
                        pe.sem_inc(seen, 1)
                        for j in range(JG):
                            m = nc.tensor.transpose(turned_p[b][:, j, 0:P], now[b][:, j, :], k.ident[0:P, 0:P])
                        m.then_inc(flipped, 1)
                        pe.wait_ge(copied, g + 1)
                        pe.wait_ge(out, i * 2)
                        for j in range(JG):
                            m = nc.tensor.matmul(made_p[b][:, j, :], turned[b][:, j, :], weight, start=True, stop=bias is None)
                            if bias is not None:
                                m = nc.tensor.matmul(made_p[b][:, j, :], k.ones[0:1, 0:P], bias, start=False, stop=True)
                        m.then_inc(made, 1)

            @block.scalar
            def _(act):
                with act.Fori(0, pairs) as i:
                    for b in range(2):
                        act.wait_ge(flipped, i * 2 + b + 1)
                        nc.scalar.copy(turned[b][:], turned_p[b][:, :, 0:P]).then_inc(copied, 1)


def norm_phase(k, x, dest):
    nc = k.nc
    with phase(nc) as ph:
        mean, var, root = (sb(k, ph, n, [P, NJ]) for n in ("mean", "var", "root"))
        cent, sq = sb(k, ph, "cent", [P, NJ, D_IN]), sb(k, ph, "sq", [P, NJ, D_IN])
        own, ready, rooted = ph.sem("own"), ph.sem("ready"), ph.sem("rooted")
        with nc.Block() as block:
            @block.vector
            def _(dve):
                c = Chain(dve, own)
                c.after(dve.tensor_reduce(mean[:], x[:], AX.X, ALU.add))
                c.after(dve.tensor_scalar(mean[:], mean[:], 1.0 / D_IN, None, ALU.mult))
                c.after(dve.tensor_tensor(cent[:], x[:], last(mean[:], D_IN), ALU.subtract))
                c.after(dve.tensor_tensor(sq[:], cent[:], cent[:], ALU.mult))
                c.after(dve.tensor_reduce(var[:], sq[:], AX.X, ALU.add))
                dve.tensor_scalar(var[:], var[:], 1.0 / D_IN, 1e-5, ALU.mult, ALU.add).then_inc(ready, 1)
                dve.wait_ge(rooted, 1)
                c.after(dve.reciprocal(root[:], root[:]))
                c.after(dve.tensor_tensor(cent[:], cent[:], last(root[:], D_IN), ALU.mult))
                dve.tensor_scalar(dest[:], cent[:], 0.0, None, ALU.max)

            @block.scalar
            def _(act):
                act.wait_ge(ready, 1)
                nc.scalar.activation(root[:], var[:], ACT.Sqrt).then_inc(rooted, 1)


def load_phase(k, dest, src):
    with phase(k.nc) as ph:
        loaded = ph.sem("loaded")
        with k.nc.Block() as block:
            @block.sync
            def _(sp):
                sp.dma_start(dest, src).then_inc(loaded, 16)
                sp.wait_ge(loaded, 16)


def dve_phase(k, body):
    nc = k.nc
    with phase(nc) as ph:
        own = ph.sem("own")
        with nc.Block() as block:
            @block.vector
            def _(dve):
                body(dve, Chain(dve, own), ph)


def elu_phase(k, v, C, bias=None, degree=None):
    nc = k.nc
    with phase(nc) as ph:
        low, d = sb(k, ph, "low", [P, NJ, C]), sb(k, ph, "d", [P, NJ])
        own, ready, exped = ph.sem("own"), ph.sem("ready"), ph.sem("exped")
        with nc.Block() as block:
            @block.vector
            def _(dve):
                c = Chain(dve, own)
                mean_and_bias(dve, c, v, C, bias, degree, d)
                dve.tensor_scalar(low[:], v[:], 0.0, None, ALU.min).then_inc(ready, 1)
                dve.wait_ge(exped, 1)
                c.after(dve.tensor_scalar(v[:], v[:], 0.0, -1.0, ALU.max, ALU.add))
                dve.tensor_tensor(v[:], v[:], low[:], ALU.add)

            @block.scalar
            def _(act):
                act.wait_ge(ready, 1)
                nc.scalar.activation(low[:], low[:], ACT.Exp).then_inc(exped, 1)


def mean_and_bias(dve, c, v, C, bias, degree, d):
    if degree is not None:
        c.after(dve.tensor_scalar(d[:], degree[:], 1.0, None, ALU.max))
        c.after(dve.reciprocal(d[:], d[:]))
        c.after(dve.tensor_tensor(v[:], v[:], last(d[:], C), ALU.mult))
    if bias is not None:
        c.after(dve.tensor_tensor(v[:], v[:], mid(bias, NJ), ALU.add))


class Table:

    def __init__(self, k, ph, src, K, weight, C, rows, side, paired, table, first=0, count=NJ):
        self.first, self.pairs = first, count // 2
        self.k, self.src, self.weight, self.C, self.rows, self.side, self.paired = k, src, weight, C, rows, side, paired
        self.cells = side - 1
        floats = self.cells * rows * 2 * C if paired else rows * side * C
        if paired:
            most = 512 // (side * C)
            self.sizes = [min(most, rows - r) * side * C for r in range(0, rows, most)]
        else:
            self.sizes = [500] * (floats // 500)
        self.starts = [sum(self.sizes[:q]) for q in range(len(self.sizes))]
        self.flat = nodes(table.rearrange("(n c) f -> n (c f)", n=N))
        self.banks = 5
        self.now = [sb(k, ph, "now", [P, K]) for _ in range(2)]
        self.turned = [sb(k, ph, "turned", [K, P]) for _ in range(2)]
        self.z = [sb(k, ph, "z", [P, floats if paired else floats // 2]) for _ in range(2)]
        self.turned_p = pb(k, ph, "turned_p", [K, 128])
        self.made_p = [pb(k, ph, f"made_p{n}", [P, 512]) for n in range(self.banks)]
        self.taken, self.seen, self.flipped, self.copied, self.made, self.out = (
            ph.sem(n) for n in ("taken", "seen", "flipped", "copied", "made", "out"))
        self.ready = ph.sem("ready")
        self.stored = [ph.sem("stored0"), ph.sem("stored1")]

    def scalar(self, act):
        nc, parts, C, side = self.k.nc, len(self.sizes), self.C, self.side
        with act.Fori(0, self.pairs) as i:
            for b in range(2):
                g = i * 2 + b
                act.wait_ge(self.flipped, g)
                nc.scalar.copy(self.now[b][:], self.src[:, bass.ds(self.first + g, 1), :].rearrange("p a k -> p (a k)")).then_inc(self.taken, 1)
                act.wait_ge(self.flipped, g + 1)
                nc.scalar.copy(self.turned[b][:], self.turned_p[:, 0:P]).then_inc(self.copied, 1)
                for q in range(parts):
                    slot = b if self.paired else q // (parts // 2)
                    if q == 0 or (not self.paired and q == parts // 2):
                        act.wait_ge(self.stored[slot], (i if self.paired else g) * 32)
                        act.sem_inc(self.seen, 1)
                    act.wait_ge(self.made, g * parts + q + 1)
                    of = self.made_p[q % self.banks][:]
                    if self.paired:
                        r, n = self.starts[q] // (side * C), self.sizes[q] // (side * C)
                        to = window(self.z[b][:], r * 2 * C, [(self.rows * 2 * C, self.cells), (2 * C, n), (1, 2 * C)])
                        of = window(of, 0, [(C, self.cells), (side * C, n), (1, 2 * C)])
                    else:
                        at = self.starts[q] - self.starts[slot * (parts // 2)]
                        to, of = self.z[slot][:, at:at + self.sizes[q]], of[:, 0:self.sizes[q]]
                    nc.scalar.copy(to, of).then_inc(self.out, 1)
                    if q == parts - 1 or (not self.paired and q == parts // 2 - 1):
                        act.wait_ge(self.out, g * parts + q + 1)
                        act.sem_inc(self.seen, 1)
                        to = self.flat[:, bass.ds(self.first + g, 1), :].rearrange("p a f -> p (a f)")
                        if not self.paired:
                            width = self.z[0].shape[1]
                            to = to[:, slot * width:(slot + 1) * width]
                        dma2(act, to, self.z[slot][:], self.stored[slot])
        for b in range(2):
            act.wait_ge(self.stored[b], self.pairs * (32 if self.paired else 64))

    def tensor(self, pe):
        nc, parts, banks = self.k.nc, len(self.sizes), self.banks
        with pe.Fori(0, self.pairs) as i:
            for b in range(2):
                g = i * 2 + b
                pe.wait_ge(self.taken, g + 1)
                pe.sem_inc(self.ready, 1)
                nc.tensor.transpose(self.turned_p[:, 0:P], self.now[b][:], self.k.ident[0:P, 0:P]).then_inc(self.flipped, 1)
                pe.wait_ge(self.copied, g + 1)
                for q in range(parts):
                    if q == 0:
                        pe.wait_ge(self.out, g * parts)
                    elif q >= banks:
                        pe.wait_ge(self.out, g * parts + q - banks + 1)
                    nc.tensor.matmul(self.made_p[q % banks][:, 0:self.sizes[q]], self.turned[b][:],
                                     self.weight[:, self.starts[q]:self.starts[q] + self.sizes[q]],
                                     start=True, stop=True).then_inc(self.made, 1)


def table_phase(k, *args):
    with phase(k.nc) as ph:
        table = Table(k, ph, *args)
        with k.nc.Block() as block:
            @block.scalar
            def _(act):
                table.scalar(act)

            @block.tensor
            def _(pe):
                table.tensor(pe)



def segment_phase(k, o, v, F, op):
    nc = k.nc
    zero = -BIG if op == ALU.max else 0.0
    rows = dram(k, "rows", [E + 1, F])
    state = sb(k, None, "state", [P, F])
    dest = sb(k, None, "segment", [P, NJ, F])
    with phase(nc) as ph:
        run, flags = sb(k, ph, "run", [P, NE, F]), sb(k, ph, "flags", [P, NE])
        own, done, stored = ph.sem("own"), ph.sem("done"), ph.sem("stored")
        with nc.Block() as block:
            @block.vector
            def _(dve):
                c = Chain(dve, own)
                if op == ALU.max:
                    c.after(dve.tensor_scalar(flags[:], o.same[:], BIG, -BIG, ALU.mult, ALU.add))
                else:
                    c.after(dve.tensor_copy(flags[:], o.same[:]))
                for f in range(F):
                    m = dve.tensor_tensor_scan(out=run[:, :, f], data0=flags[:], data1=v[:, :, f], initial=zero,
                                               op0=ALU.add if op == ALU.max else ALU.mult, op1=op)
                c.after(m)
                dve.tensor_copy(state[:], run[:, NE - 1, :]).then_inc(done, 1)

            @block.sync
            def _(sp):
                sp.wait_ge(done, 1)
                dma2(sp, edges(rows), run[:], stored)
                sp.wait_ge(stored, 32)
    carry_phase(k, o, state, F, rows, op, zero)
    collect_phase(k, o, rows, F, dest)
    return dest


def expand_phase(k, o, src, F, dest):
    nc = k.nc
    spread, head, _ = scatter_nodes_phase(k, o, src, F)
    with phase(nc) as ph:
        loaded, own = ph.sem("loaded"), ph.sem("own")
        first = sb(k, ph, "first", [P, NE, F])
        with nc.Block() as block:
            @block.sync
            def _(sp):
                dma2(sp, first[:], edges(spread), loaded)

            @block.vector
            def _(dve):
                dve.wait_ge(loaded, 32)
                for f in range(F):
                    dve.tensor_tensor_scan(out=dest[:, :, f], data0=o.same[:], data1=first[:, :, f],
                                           initial=head[:, f:f + 1], op0=ALU.mult, op1=ALU.add)


@contextmanager
def layer(k):
    outer = k.ctx
    with ExitStack() as ctx:
        k.ctx = ctx
        yield
    k.ctx = outer


def add_phase(k, dest, other):
    def body(dve, c, ph):
        dve.tensor_tensor(dest[:], dest[:], other[:], ALU.add)
    dve_phase(k, body)


def aggregate(k, o, table, index, F, dest, beside, T):
    rows = dram(k, "rows", [E + 1, F])

    def work(dve, c, at, got, read, tmp, res, exp):
        return got[0]
    state = edge_pass(k, o, T, [(table, index, F)], [], F, work, 0, out=rows, beside=beside)
    carry_phase(k, o, state, F, rows)
    collect_phase(k, o, rows, F, dest)


def column_of(array):
    return lambda at: array[:, at, :].rearrange("p t a -> p (t a)")



def gin_layer(k, o, x, w, beside):
    with layer(k):
        h, y = sb(k, None, "h", [P, NJ, D_IN]), sb(k, None, "y", [P, NJ, D_IN])
        source = column_of(o.kept[0])
        norm_phase(k, x, h)
        aggregate(k, o, store_nodes_phase(k, h, D_IN), source, D_IN, y, beside[0], 50)
        add_phase(k, y, h)
        a, b = sb(k, None, "a", [P, NJ, D_HID]), sb(k, None, "b", [P, NJ, D_HID])
        dense_phase(k, y, D_IN, w["W1a"][:], D_HID, a, w["b1a"][:], relu=True)
        dense_phase(k, a, D_HID, w["W2a"][:], D_HID, b, w["b2a"][:], relu=True)
        aggregate(k, o, store_nodes_phase(k, b, D_HID), source, D_HID, a, beside[1], 40)
        add_phase(k, a, b)
        dense_phase(k, a, D_HID, w["W1b"][:], D_HID, b, w["b1b"][:], relu=True)
        dense_phase(k, b, D_HID, w["W2b"][:], D_IN, y, w["b2b"][:])
        add_phase(k, x, y)


def attention_layer(k, o, x, w, r_feat):
    with layer(k):
        h, y = sb(k, None, "h", [P, NJ, D_IN]), sb(k, None, "y", [P, NJ, D_IN])
        e = sb(k, None, "e", [P, NE, HEADS])
        alpha = sb(k, None, "alpha", [P, NE, HEADS])
        en_rows = dram(k, "en_rows", [E, D_HID])
        norm_phase(k, x, h)
        with layer(k):
            a = sb(k, None, "a", [P, NJ, D_HID])
            dense_phase(k, h, D_IN, w["W2s"][:], D_HID, a, w["b2s"][:])
            sources = store_nodes_phase(k, a, D_HID)
            dense_phase(k, h, D_IN, w["W2d"][:], D_HID, a, w["b2d"][:])
            spread, head, _ = scatter_nodes_phase(k, o, a, D_HID)
            T = 50

            def scores(dve, c, at, got, read, tmp, res, exp):
                s, t = tmp
                for f in range(D_HID):
                    m = dve.tensor_tensor_scan(out=s[:, :, f], data0=o.same[:, at], data1=read[0][:, :, f],
                                               initial=head[:, f:f + 1], op0=ALU.mult, op1=ALU.add)
                c.after(m)
                c.after(dve.tensor_copy(head[:], s[:, T - 1, :]))
                c.after(dve.tensor_tensor(s[:], s[:], got[0][:], ALU.add))
                c.after(dve.scalar_tensor_tensor(t[:], s[:], 0.2, s[:], ALU.mult, ALU.max))
                c.after(dve.tensor_tensor(t[:], t[:], mid(w["attn"][:], T), ALU.mult))
                c.after(dve.tensor_reduce(e[:, at, :], t[:].rearrange("p t (h f) -> p t h f", h=HEADS), AX.X, ALU.add))
            edge_pass(k, o, T, [(sources, column_of(o.kept[0]), D_HID)], [(spread, D_HID)], 0, scores, 6,
                      keep=(0, en_rows), extra=[[D_HID], [D_HID]])

        expand_phase(k, o, segment_phase(k, o, e, HEADS, ALU.max), HEADS, alpha)
        nc = k.nc
        with phase(nc) as ph:
            own, exped = ph.sem("own"), ph.sem("exped")
            with nc.Block() as block:
                @block.vector
                def _(dve):
                    dve.tensor_tensor(e[:], e[:], alpha[:], ALU.subtract).then_inc(own, 1)

                @block.scalar
                def _(act):
                    act.wait_ge(own, 1)
                    nc.scalar.activation(e[:], e[:], ACT.Exp).then_inc(exped, 1)
        expand_phase(k, o, segment_phase(k, o, e, HEADS, ALU.add), HEADS, alpha)

        def divide(dve, c, ph):
            c.after(dve.tensor_scalar(alpha[:], alpha[:], 1e-9, None, ALU.max))
            c.after(dve.reciprocal(alpha[:], alpha[:]))
            dve.tensor_tensor(alpha[:], alpha[:], e[:], ALU.mult)
        dve_phase(k, divide)

        def messages(dve, c, at, got, read, tmp, res, exp):
            m, red, both = tmp
            v = m[:].rearrange("p t (h f) -> p (t h) f", h=HEADS)
            heads = red[:].rearrange("p t h -> p (t h)")
            to_exp, exped, n = exp
            c.after(dve.tensor_tensor(m[:], read[0][:], got[0][:], ALU.mult))
            c.after(dve.tensor_tensor(m[:].rearrange("p t (h f) -> p t h f", h=HEADS),
                                      m[:].rearrange("p t (h f) -> p t h f", h=HEADS),
                                      last(alpha[:, at, :], D_IN), ALU.mult))
            c.after(dve.tensor_reduce(heads, v, AX.X, ALU.max))
            dve.tensor_tensor(v, v, last(heads, D_IN), ALU.subtract).then_inc(to_exp, 1)
            dve.wait_ge(exped, n)
            c.after(dve.tensor_reduce(heads, v, AX.X, ALU.add))
            c.after(dve.reciprocal(red[:], red[:]))
            c.after(dve.tensor_tensor(v, v, last(heads, D_IN), ALU.mult))
            c.after(dve.tensor_tensor(both[:], m[:, :, 0:D_IN], m[:, :, D_IN:], ALU.add))
            return both
        rows = dram(k, "rows", [E + 1, D_IN])
        state = edge_pass(k, o, 50, [(r_feat, column_of(o.kept[1]), D_HID)], [(en_rows, D_HID)], D_IN, messages, 7,
                          out=rows, extra=[[D_HID], [HEADS], [D_IN]], exp_of=0)
        carry_phase(k, o, state, D_IN, rows)
        collect_phase(k, o, rows, D_IN, y)
        add_phase(k, h, y)
        dense_phase(k, h, D_IN, w["W1"][:], D_IN, y, w["b1"][:])
        add_phase(k, x, y)


def floor_clipped(dve, c, pos, clipped, q_i, top):
    c.after(dve.tensor_scalar(clipped, pos, 0.0, float(top), ALU.max, ALU.min))
    c.after(dve.tensor_copy(q_i[0], clipped))
    c.after(dve.tensor_copy(q_i[1], q_i[0]))
    c.after(dve.tensor_tensor(q_i[2], q_i[1], clipped, ALU.is_gt))
    c.after(dve.tensor_tensor(clipped, q_i[1], q_i[2], ALU.subtract))


def tent_layer(k, o, x, w):
    with layer(k):
        h, y = sb(k, None, "h", [P, NJ, D_IN]), sb(k, None, "y", [P, NJ, D_IN])
        norm_phase(k, x, h)
        table = dram(k, "patches", [N * 12, 2 * D_IN])
        table_phase(k, h, D_IN, w["tent_w"], D_IN, 4, 4, True, table)
        weights, index = sb(k, None, "weights", [P, NE, 4]), sb(k, None, "index", [P, NE], I32)
        uv = o.kept[1]

        def basis(dve, c, ph):
            pos, cell, q, g = (sb(k, ph, n, [P, NE, 2]) for n in ("pos", "cell", "q", "g"))
            q_i = sb(k, ph, "q_i", [P, NE, 2], I32)
            tents = [sb(k, ph, "tent", [P, NE, 2]) for _ in range(2)]
            flat = sb(k, ph, "flat", [P, NE])
            c.after(dve.tensor_scalar(pos[:], uv[:], 1.0, 1.5, ALU.add, ALU.mult))
            floor_clipped(dve, c, pos[:], cell[:], (q_i[:], q[:], g[:]), 2.5)
            for n in range(2):
                c.after(dve.tensor_scalar(q[:], cell[:], 2.0 / 3.0, -1.0 + n * 2.0 / 3.0, ALU.mult, ALU.add))
                c.after(dve.tensor_tensor(q[:], uv[:], q[:], ALU.subtract))
                c.after(dve.scalar_tensor_tensor(g[:], q[:], -1.0, q[:], ALU.mult, ALU.max))
                c.after(dve.tensor_scalar(g[:], g[:], -1.5, 1.0, ALU.mult, ALU.add))
                c.after(dve.tensor_scalar(tents[n][:], g[:], 0.0, None, ALU.max))
            for a in range(2):
                for b in range(2):
                    dve.tensor_tensor(weights[:, :, 2 * a + b], tents[a][:, :, 0], tents[b][:, :, 1], ALU.mult)
            c.after(dve.tensor_copy(flat[:], o.kept[0][:, :, 0]))
            c.after(dve.scalar_tensor_tensor(flat[:], flat[:], 3.0, cell[:, :, 1], ALU.mult, ALU.add))
            c.after(dve.scalar_tensor_tensor(flat[:], flat[:], 4.0, cell[:, :, 0], ALU.mult, ALU.add))
            dve.tensor_copy(index[:], flat[:])
        dve_phase(k, basis)
        rows = dram(k, "rows", [E + 1, D_IN])

        def work(dve, c, at, got, read, tmp, res, exp):
            v = got[0][:].rearrange("p t (c f) -> p t c f", c=4)
            c.after(dve.tensor_tensor(v, v, last(weights[:, at, :], D_IN), ALU.mult))
            c.after(dve.tensor_reduce(tmp[0][:], got[0][:].rearrange("p t (c f) -> p t f c", c=4), AX.X, ALU.add))
            return tmp[0]
        state = edge_pass(k, o, 50, [(table, lambda at: index[:, at], 4 * D_IN)], [], D_IN, work, 2, out=rows,
                          extra=[[D_IN]])
        carry_phase(k, o, state, D_IN, rows)
        collect_phase(k, o, rows, D_IN, y)
        add_phase(k, x, y)


def spline_basis(k, pseudo, whole, frac, rest):
    def body(dve, c, ph):
        q, g = sb(k, ph, "q", [P, NE, 3]), sb(k, ph, "g", [P, NE, 3])
        q_i = sb(k, ph, "q_i", [P, NE, 3], I32)
        c.after(dve.tensor_scalar(frac[:], pseudo[:], 4.0, None, ALU.mult))
        floor_clipped(dve, c, frac[:], whole[:], (q_i[:], q[:], g[:]), 3)
        c.after(dve.tensor_tensor(frac[:], frac[:], whole[:], ALU.subtract))
        dve.tensor_scalar(rest[:], frac[:], -1.0, 1.0, ALU.mult, ALU.add)
    dve_phase(k, body)


SPAN = 7


class Convolution:

    def __init__(self, k, K, C, paired):
        self.K, self.C, self.paired = K, C, paired
        self.unit, self.gathers = (2 * C, 1) if paired else (C, 2)
        self.table = dram(k, "corners", [N * (4 * 25 if paired else K3), self.unit])

    def making(self, k, h, weight):
        K, C = self.K, self.C
        loaded_weight = sb(k, None, "conv_weight", [K, K3 * C])
        load_phase(k, loaded_weight[:].rearrange("p (a b) -> p a b", a=K3), weight)
        if self.paired:
            turned_weight = sb(k, None, "turned_weight", [K, K3 * C])

            def permute(dve, c, ph):
                dve.tensor_copy(turned_weight[:].rearrange("p (s g q) -> p g s q", s=5, g=5),
                                loaded_weight[:].rearrange("p (g s q) -> p g s q", s=5, g=5))
            dve_phase(k, permute)
            loaded_weight = turned_weight
        return h, K, loaded_weight, C, 25, 5, self.paired, self.table


def spline_conv(k, o, conv, pseudo, dest, T):
    C, paired, unit, gathers, table = conv.C, conv.paired, conv.unit, conv.gathers, conv.table
    with layer(k):
        index = [sb(k, None, "index", [P, NE], I32) for _ in range(gathers)]
        weight_rows = dram(k, "corner_weights", [E, 8])
        with layer(k):
            weights = sb(k, None, "weights", [P, NE, 8])
            whole, frac, rest = (sb(k, None, n, [P, NE, 3]) for n in ("whole", "frac", "rest"))
            spline_basis(k, pseudo, whole, frac, rest)

            def corners(dve, c, ph):
                pair, flat = sb(k, ph, "pair", [P, NE, 4]), sb(k, ph, "flat", [P, NE])
                side = (rest, frac)
                for b in range(2):
                    for d in range(2):
                        m = dve.tensor_tensor(pair[:, :, 2 * b + d], side[b][:, :, 1], side[d][:, :, 2], ALU.mult)
                c.after(m)
                for a in range(2):
                    dve.tensor_tensor(weights[:, :, 4 * a:4 * a + 4], pair[:], last(side[a][:, :, 0], 4), ALU.mult)
                c.after(dve.tensor_copy(flat[:], o.kept[0][:, :, 0]))
                for scale, d in ((4.0, 2), (5.0, 1), (5.0, 0)) if paired else ((5.0, 0), (5.0, 1), (5.0, 2)):
                    c.after(dve.scalar_tensor_tensor(flat[:], flat[:], scale, whole[:, :, d], ALU.mult, ALU.add))
                for a in range(gathers):
                    dve.tensor_scalar(index[a][:], flat[:], 25.0 * a, None, ALU.add)
            dve_phase(k, corners)
            load_phase(k, edges(weight_rows), weights[:])
        rows = dram(k, "rows", [E + 1, C])

        def work(dve, c, at, got, read, tmp, res, exp):
            for a in range(2):
                for b in range(2):
                    g = got[0 if paired else a]
                    first = b * 5 + a if paired else b * 5
                    v = window(g[:], first * unit, [(SPAN * unit, T), (C, 2), (1, C)])
                    of = last(read[0][:, :, 4 * a + 2 * b:4 * a + 2 * b + 2], C)
                    m = dve.tensor_tensor(v, v, of, ALU.mult)
            c.after(m)

            def corner(a, b, d):
                first = b * 5 + a if paired else b * 5
                return window(got[0 if paired else a][:], first * unit + d * C, [(SPAN * unit, T), (1, C)])
            for a in range(2):
                for b in range(2):
                    m = dve.tensor_tensor(corner(a, b, 0), corner(a, b, 0), corner(a, b, 1), ALU.add)
            c.after(m)
            for a in range(2):
                m = dve.tensor_tensor(corner(a, 0, 0), corner(a, 0, 0), corner(a, 1, 0), ALU.add)
            c.after(m)
            c.after(dve.tensor_tensor(corner(0, 0, 0), corner(0, 0, 0), corner(1, 0, 0), ALU.add))
            first = got[0][:]
            return first[:, :, 0:C]
        tables = [(table, lambda at, a=a: index[a][:, at], SPAN * unit) for a in range(gathers)]
        state = edge_pass(k, o, T, tables, [(weight_rows, 8)], C, work, 4, out=rows)
        carry_phase(k, o, state, C, rows)
        collect_phase(k, o, rows, C, dest)


def spline_first(k, o, v, w):
    with layer(k):
        pseudo = o.kept[2]
        with layer(k):
            whole, frac, rest = (sb(k, None, n, [P, NE, 3]) for n in ("whole", "frac", "rest"))
            spline_basis(k, pseudo, whole, frac, rest)
            sums = sb(k, None, "sums", [P, NJ, K3])
            rows = dram(k, "rows", [E + 1, K3])
            T = 25

            def work(dve, c, at, got, read, tmp, res, exp):
                u, u1, pair, full = tmp
                five = k.column[0:P, 0:5].unsqueeze(1).unsqueeze(1).broadcast_to([P, T, 3, 5])
                under = k.column_less[0:P, 0:5].unsqueeze(1).unsqueeze(1).broadcast_to([P, T, 3, 5])
                dve.tensor_tensor(u[:], five, last(whole[:, at, :], 5), ALU.is_equal)
                c.after(dve.tensor_tensor(u1[:], under, last(whole[:, at, :], 5), ALU.is_equal))
                dve.tensor_tensor(u[:], u[:], last(rest[:, at, :], 5), ALU.mult)
                c.after(dve.tensor_tensor(u1[:], u1[:], last(frac[:, at, :], 5), ALU.mult))
                c.after(dve.tensor_tensor(u[:], u[:], u1[:], ALU.add))
                c.after(dve.tensor_tensor(pair[:], last(u[:, :, 0, :], 5),
                                          u[:, :, 1, :].unsqueeze(2).broadcast_to([P, T, 5, 5]), ALU.mult))
                c.after(dve.tensor_tensor(full[:], last(pair[:].rearrange("p t a b -> p t (a b)"), 5),
                                          u[:, :, 2, :].unsqueeze(2).broadcast_to([P, T, 25, 5]), ALU.mult))
                return full[:].rearrange("p t a b -> p t (a b)")
            state = edge_pass(k, o, T, [], [], K3, work, 5, out=rows, extra=[[3, 5], [3, 5], [5, 5], [25, 5]])
            carry_phase(k, o, state, K3, rows)
            collect_phase(k, o, rows, K3, sums)
            dense_phase(k, sums, K3, w["stn1_w"][:], D_HID, v)
        elu_phase(k, v, D_HID, w["stn1_b"][0:P], o.degree)


def spline_layer(k, o, x, v, conv, w):
    with layer(k):
        h, y = sb(k, None, "h", [P, NJ, D_IN]), sb(k, None, "y", [P, NJ, D_IN])
        pseudo = o.kept[2]
        norm_phase(k, x, h)
        spline_conv(k, o, conv, pseudo, v, 16)
        last_conv = Convolution(k, D_IN, D_IN, True)
        elu_phase(k, v, D_HID, w["stn2_b"][0:P], o.degree)
        with layer(k):
            u, t = sb(k, None, "u", [P, NJ, D_HID]), sb(k, None, "t", [P, NJ, 3])
            here, there = sb(k, None, "here", [P, NE, 3]), sb(k, None, "there", [P, NE, 3])
            dense_phase(k, v, D_HID, w["stn3_w"][:], D_HID, u, w["stn3_b"][:])
            elu_phase(k, u, D_HID)
            dense_phase(k, u, D_HID, w["stn4_w"][:], 3, t, w["stn4_b"][:])
            expand_phase(k, o, t, 3, here)
            table = store_nodes_phase(k, t, 3)

            def take(dve, c, at, got, read, tmp, res, exp):
                c.after(dve.tensor_copy(there[:, at, :], got[0][:]))
            edge_pass(k, o, 50, [(table, column_of(o.kept[0]), 3)], [], 0, take, 1,
                      beside=last_conv.making(k, h, k.conv_w))

            def shift(dve, c, ph):
                c.after(dve.tensor_tensor(pseudo[:], pseudo[:], there[:], ALU.add))
                c.after(dve.tensor_tensor(pseudo[:], pseudo[:], here[:], ALU.subtract))
                dve.tensor_scalar(pseudo[:], pseudo[:], 0.0, 1.0, ALU.max, ALU.min)
            dve_phase(k, shift)
        spline_conv(k, o, last_conv, pseudo, y, 20)

        def finish(dve, c, ph):
            mean_and_bias(dve, c, y, D_IN, w["conv_b"][0:P], o.degree, sb(k, ph, "d", [P, NJ]))
            dve.tensor_tensor(x[:], x[:], y[:], ALU.add)
        dve_phase(k, finish)


def program(nc, x, src, dst, edge_attr3_2x32, edge_attr_2, edge_attr_3, W1a, b1a, W2a, b2a, W1b, b1b, W2b, b2b,
            W1, b1, W2s, b2s, W2d, b2d, attn, tent_w, stn1_w, stn1_b, stn2_w, stn2_b, stn3_w, stn3_b,
            stn4_w, stn4_b, conv_w, conv_b, out, layers=4):
    k = Scope(None)
    k.nc = nc
    with ExitStack() as ctx:
        k.ctx = ctx
        as_row = lambda v: v.unsqueeze(0)
        weights = {
            "W1a": W1a, "b1a": as_row(b1a), "W2a": W2a, "b2a": as_row(b2a), "W1b": W1b, "b1b": as_row(b1b),
            "W2b": W2b, "b2b": as_row(b2b), "W1": W1, "b1": as_row(b1), "W2s": W2s, "b2s": as_row(b2s),
            "W2d": W2d, "b2d": as_row(b2d), "attn": across(attn.rearrange("a h f -> (a h f)"), P),
            "tent_w": tent_w.rearrange("a b i o -> i (a b) o"), "stn1_w": stn1_w.rearrange("k a o -> k (a o)"),
            "stn1_b": across(stn1_b, P), "stn2_b": across(stn2_b, P),
            "stn3_w": stn3_w, "stn3_b": as_row(stn3_b), "stn4_w": stn4_w, "stn4_b": as_row(stn4_b),
            "conv_b": across(conv_b, P),
        }
        constants_phase(k, weights)
        k.stn2_w, k.conv_w = stn2_w.rearrange("k i o -> i k o"), conv_w.rearrange("k i o -> i k o")
        xs = sb(k, None, "xs", [P, NJ, D_IN])
        with phase(nc) as ph:
            loaded = ph.sem("loaded")
            with nc.Block() as block:
                @block.sync
                def _(sp):
                    dma2(sp, xs[:], nodes(x), loaded)
                    sp.wait_ge(loaded, 32)
        one = lambda v: v.rearrange("(e a) -> e a", a=1)
        by_src = sort_edges(k, src, 8, [(one(src), 1, I32, 0), (one(dst), 1, I32, 1), (edge_attr_2, 2, F32, 2),
                                        (edge_attr_3, 3, F32, 4)])
        from_src = make_order(k, *by_src, 8, [(1, 1, I32), (2, 2, F32), (4, 3, F32)])
        v = sb(k, None, "v", [P, NJ, D_HID])
        spline_first(k, from_src, v, k.w)
        conv = Convolution(k, D_HID, D_HID, False)
        by_dst = sort_edges(k, dst, 4, [(one(dst), 1, I32, 0), (one(src), 1, I32, 1), (None, 1, I32, 2)])
        with layer(k):
            o = make_order(k, *by_dst, 4, [(1, 1, I32), (2, 1, I32)])
            with layer(k):
                args = conv.making(k, v, k.stn2_w)
                gin_layer(k, o, xs, k.w, [(*args, 0, NJ // 2 + 1), (*args, NJ // 2 + 1, NJ // 2 - 1)])
            if layers > 1:
                attention_layer(k, o, xs, k.w, edge_attr3_2x32.rearrange("e h f -> e (h f)"))
        if layers > 2:
            tent_layer(k, from_src, xs, k.w)
        if layers > 3:
            spline_layer(k, from_src, xs, v, conv, k.w)
        with phase(nc) as ph:
            stored = ph.sem("stored")
            with nc.Block() as block:
                @block.sync
                def _(sp):
                    dma2(sp, nodes(out), xs[:], stored)
                    sp.wait_ge(stored, 32)


_INS = ["x", "src", "dst", "edge_attr3_2x32", "edge_attr_2", "edge_attr_3",
        "L0_gnn_W1a", "L0_gnn_b1a", "L0_gnn_W2a", "L0_gnn_b2a", "L0_gnn_W1b", "L0_gnn_b1b", "L0_gnn_W2b", "L0_gnn_b2b",
        "L1_gnn_W1", "L1_gnn_b1", "L1_gnn_W2s", "L1_gnn_b2s", "L1_gnn_W2d", "L1_gnn_b2d", "L1_gnn_attn",
        "L2_gnn_weight", "L3_gnn_stn1_w", "L3_gnn_stn1_b", "L3_gnn_stn2_w", "L3_gnn_stn2_b", "L3_gnn_stn3_w",
        "L3_gnn_stn3_b", "L3_gnn_stn4_w", "L3_gnn_stn4_b", "L3_gnn_conv_w", "L3_gnn_conv_b"]


def kernel(**inputs):
    import numpy as _np
    import concourse.bacc as _bacc
    from concourse import mybir as _mybir
    from concourse.bass_utils import run_bass_kernel_spmd as _run

    nc = _bacc.Bacc("TRN2", target_bir_lowering=False, num_devices=1)
    arrays, args = {}, []
    for name in _INS:
        a = _np.ascontiguousarray(inputs[name])
        arrays[f"in_{name}_dram"] = a
        args.append(nc.dram_tensor(f"in_{name}_dram", a.shape, _mybir.dt.from_np(a.dtype), kind="ExternalInput").ap())
    args.append(nc.dram_tensor("out_dram", (N, D_IN), F32, kind="ExternalOutput").ap())
    program(nc, *args)
    r = _run(nc, [arrays], core_ids=[0])
    return r.results[0]["out_dram"]
```
